# Optimizing a Trainium2 kernel written in Bass

```python
import numpy as np
import jax
import jax.numpy as jnp

def _softmax(x, axis=-1):
    return jax.nn.softmax(x, axis=axis)

def _gelu(x):
    return jax.nn.gelu(x, approximate=True)

def _silu(x):
    return jax.nn.silu(x)

def _sigmoid(x):
    return jax.nn.sigmoid(x)

def _layernorm(x, axis=-1, eps=1e-05):
    m = jnp.mean(x, axis=axis, keepdims=True)
    v = jnp.var(x, axis=axis, keepdims=True)
    return (x - m) / jnp.sqrt(v + eps)

def _scatter_add(tgt, idx, src, axis=0):
    return tgt.at[idx].add(src)

def _segment_sum(src, seg, n):
    return jax.ops.segment_sum(src, seg, n)
kernel_name = 'mk_gnn_preln_d4_gnn_r8_e4d347'

def setup_inputs(seed: int=0):
    np.random.seed(seed)
    _w = jnp.asarray

    def _rec_inputs():
        import jax
        import jax.numpy as jnp
        _gk = jax.random.key(seed)
        x = -0.0009044 + 1 * jax.random.normal(jax.random.fold_in(_gk, 1), (12500, 16), jnp.float32)
        _s = jax.random.randint(jax.random.fold_in(_gk, 2), (200000,), 0, 12500, jnp.int32)
        _d = jax.random.randint(jax.random.fold_in(_gk, 3), (200000,), 0, 12500, jnp.int32)
        _loop = jnp.arange(12500, dtype=jnp.int32)
        src = jnp.concatenate([_s, _d, _loop])
        dst = jnp.concatenate([_d, _s, _loop])
        _o = jnp.argsort(dst, stable=True)
        src = src[_o]
        dst = dst[_o]
        edge_attr_16 = 0.000189758 + 1.00013 * jax.random.normal(jax.random.fold_in(_gk, 12), (412500, 16), jnp.float32)
        edge_type_90 = jax.random.randint(jax.random.fold_in(_gk, 14), (412500,), 0, 90, jnp.int32)
        return (x, src, dst, edge_attr_16, edge_type_90)
    x, src, dst, edge_attr_16, edge_type_90 = _rec_inputs()

    def _L0_gnn_setup():
        import jax, jax.numpy as jnp
        import numpy as np
        N = 12500
        E = 100000
        F_IN = 16
        H1, C1 = (3, 32)
        H2, C2 = (1, 32)
        NC = 16
        SLOPE = 0.2

        def _gat_layer(x, src, dst, W, a_s, a_d, b, heads, outc):
            h = (x @ W).reshape(N, heads, outc)
            alpha_s = (h * a_s).sum(-1)
            alpha_d = (h * a_d).sum(-1)
            e = jax.nn.leaky_relu(alpha_s[src] + alpha_d[dst], SLOPE)
            m = jax.ops.segment_max(e, dst, num_segments=N)
            p = jnp.exp(e - m[dst])
            z = jax.ops.segment_sum(p, dst, num_segments=N)
            alpha = p / (z[dst] + 1e-16)
            out = jax.ops.segment_sum(h[src] * alpha[:, :, None], dst, num_segments=N)
            return out.reshape(N, heads * outc) + b
        key = jax.random.key(seed)
        ks = jax.random.split(key, 12)
        s = 0.1
        return {'x': jax.random.normal(ks[0], (N, F_IN), jnp.float32), 'edge_index': jax.random.randint(ks[1], (2, E), 0, N, dtype=jnp.int32), 'W1': jax.random.normal(ks[2], (F_IN, H1 * C1), jnp.float32) * s, 'a_src1': jax.random.normal(ks[3], (H1, C1), jnp.float32) * s, 'a_dst1': jax.random.normal(ks[4], (H1, C1), jnp.float32) * s, 'b1': jnp.zeros((H1 * C1,), jnp.float32), 'W2': jax.random.normal(ks[5], (H1 * C1, H2 * C2), jnp.float32) * s, 'a_src2': jax.random.normal(ks[6], (H2, C2), jnp.float32) * s, 'a_dst2': jax.random.normal(ks[7], (H2, C2), jnp.float32) * s, 'b2': jnp.zeros((H2 * C2,), jnp.float32), 'Wf': jax.random.normal(ks[8], (C2, NC), jnp.float32) * s, 'bf': jnp.zeros((NC,), jnp.float32)}
    _L0_gnn_all = _L0_gnn_setup()
    _L0_gnn_in = {k: v for k, v in _L0_gnn_all.items() if k in ('W1', 'a_src1', 'a_dst1', 'b1', 'W2', 'a_src2', 'a_dst2', 'b2', 'Wf', 'bf')}
    del _L0_gnn_all

    def _L1_gnn_setup():
        import jax, jax.numpy as jnp
        import numpy as np
        N_NODES = 12500
        N_EDGES = 400000
        D_FEAT = 16
        key = jax.random.key(seed)
        k1, k2, k3 = jax.random.split(key, 3)
        x = jax.random.normal(k1, (N_NODES, D_FEAT), dtype=jnp.float32)
        edge_index = jax.random.randint(k2, (2, N_EDGES), 0, N_NODES, dtype=jnp.int64)
        edge_attr = jax.random.normal(k3, (N_EDGES, D_FEAT), dtype=jnp.float32)
        return {'x': x, 'edge_index': edge_index, 'edge_attr': edge_attr}
    _L1_gnn_all = _L1_gnn_setup()
    _L1_gnn_in = {k: v for k, v in _L1_gnn_all.items() if k in ()}
    del _L1_gnn_all

    def _L2_gnn_setup():
        import jax, jax.numpy as jnp
        import numpy as np
        N, E, IN, OUT, R, B = (6250, 100000, 16, 16, 90, 30)
        key = jax.random.key(seed)
        ks = jax.random.split(key, 9)
        h = jax.random.normal(ks[0], (N, IN), dtype=jnp.float32)
        he = jax.random.normal(ks[1], (E, IN), dtype=jnp.float32)
        Ws = jax.random.normal(ks[2], (OUT, IN), dtype=jnp.float32) * 0.1
        Wa = jax.random.normal(ks[3], (1, 3 * OUT), dtype=jnp.float32) * 0.1
        weight = jax.random.normal(ks[4], (B, IN, OUT), dtype=jnp.float32) * 0.1
        w_comp = jax.random.normal(ks[5], (R, B), dtype=jnp.float32) * 0.1
        src = jax.random.randint(ks[6], (E,), 0, N)
        dst = jax.random.randint(ks[7], (E,), 0, N)
        rel_type = jax.random.randint(ks[8], (E,), 0, R)
        return {'h': h, 'he': he, 'Ws': Ws, 'Wa': Wa, 'weight': weight, 'w_comp': w_comp, 'src': src, 'dst': dst, 'rel_type': rel_type}
    _L2_gnn_all = _L2_gnn_setup()
    _L2_gnn_in = {k: v for k, v in _L2_gnn_all.items() if k in ('Ws', 'Wa', 'weight', 'w_comp')}
    del _L2_gnn_all

    def _L3_gnn_setup():
        import jax, jax.numpy as jnp
        import numpy as np
        N_NODES = 125000
        key = jax.random.key(seed)
        k1, k2, k3 = jax.random.split(key, 3)
        x = jax.random.normal(k1, (N_NODES, 16), dtype=jnp.float32)
        edge_index = jax.random.randint(k2, (2, 500000), 0, N_NODES, dtype=jnp.int64)
        W = jax.random.normal(k3, (16, 16), dtype=jnp.float32) * (1.0 / np.sqrt(16.0))
        b = jnp.zeros((16,), dtype=jnp.float32)
        return {'x': x, 'edge_index': edge_index, 'W': W, 'b': b}
    _L3_gnn_all = _L3_gnn_setup()
    _L3_gnn_in = {k: v for k, v in _L3_gnn_all.items() if k in ('W', 'b')}
    del _L3_gnn_all
    return {'x': x, 'src': src, 'dst': dst, 'edge_attr_16': edge_attr_16, 'edge_type_90': edge_type_90, 'L0_gnn_W1': _L0_gnn_in['W1'], 'L0_gnn_a_src1': _L0_gnn_in['a_src1'], 'L0_gnn_a_dst1': _L0_gnn_in['a_dst1'], 'L0_gnn_b1': _L0_gnn_in['b1'], 'L0_gnn_W2': _L0_gnn_in['W2'], 'L0_gnn_a_src2': _L0_gnn_in['a_src2'], 'L0_gnn_a_dst2': _L0_gnn_in['a_dst2'], 'L0_gnn_b2': _L0_gnn_in['b2'], 'L0_gnn_Wf': _L0_gnn_in['Wf'], 'L0_gnn_bf': _L0_gnn_in['bf'], 'L2_gnn_Ws': _L2_gnn_in['Ws'], 'L2_gnn_Wa': _L2_gnn_in['Wa'], 'L2_gnn_weight': _L2_gnn_in['weight'], 'L2_gnn_w_comp': _L2_gnn_in['w_comp'], 'L3_gnn_W': _L3_gnn_in['W'], 'L3_gnn_b': _L3_gnn_in['b']}

def reference(x, src, dst, edge_attr_16, edge_type_90, L0_gnn_W1, L0_gnn_a_src1, L0_gnn_a_dst1, L0_gnn_b1, L0_gnn_W2, L0_gnn_a_src2, L0_gnn_a_dst2, L0_gnn_b2, L0_gnn_Wf, L0_gnn_bf, L2_gnn_Ws, L2_gnn_Wa, L2_gnn_weight, L2_gnn_w_comp, L3_gnn_W, L3_gnn_b):
    import jax
    import jax.numpy as jnp

    def _L0_gnn_ref(x, edge_index, W1, a_src1, a_dst1, b1, W2, a_src2, a_dst2, b2, Wf, bf):
        import jax, jax.numpy as jnp
        import numpy as np
        N = 12500
        E = 100000
        F_IN = 16
        H1, C1 = (3, 32)
        H2, C2 = (1, 32)
        NC = 16
        SLOPE = 0.2

        def _gat_layer(x, src, dst, W, a_s, a_d, b, heads, outc):
            h = (x @ W).reshape(N, heads, outc)
            alpha_s = (h * a_s).sum(-1)
            alpha_d = (h * a_d).sum(-1)
            e = jax.nn.leaky_relu(alpha_s[src] + alpha_d[dst], SLOPE)
            m = jax.ops.segment_max(e, dst, num_segments=N)
            p = jnp.exp(e - m[dst])
            z = jax.ops.segment_sum(p, dst, num_segments=N)
            alpha = p / (z[dst] + 1e-16)
            out = jax.ops.segment_sum(h[src] * alpha[:, :, None], dst, num_segments=N)
            return out.reshape(N, heads * outc) + b
        loops = jnp.arange(N, dtype=edge_index.dtype)
        src = jnp.concatenate([edge_index[0], loops])
        dst = jnp.concatenate([edge_index[1], loops])
        h = jax.nn.selu(_gat_layer(x, src, dst, W1, a_src1, a_dst1, b1, H1, C1))
        h = jax.nn.selu(_gat_layer(h, src, dst, W2, a_src2, a_dst2, b2, H2, C2))
        return h @ Wf + bf

    def _L1_gnn_ref(x, edge_index, edge_attr):
        import jax, jax.numpy as jnp
        import numpy as np
        N_NODES = 12500
        N_EDGES = 400000
        D_FEAT = 16
        nb_node = x.shape[0]
        dst = edge_index[1]
        sums = jax.ops.segment_sum(edge_attr, dst, num_segments=nb_node)
        counts = jax.ops.segment_sum(jnp.ones((edge_attr.shape[0],), dtype=edge_attr.dtype), dst, num_segments=nb_node)
        denom = jnp.where(counts > 0, counts, jnp.ones_like(counts))
        return sums / denom[:, None]

    def _L2_gnn_ref(h, he, Ws, Wa, weight, w_comp, src, dst, rel_type):
        import jax, jax.numpy as jnp
        import numpy as np
        N, E, IN, OUT, R, B = (6250, 100000, 16, 16, 90, 30)
        n_nodes, in_dim = h.shape
        num_bases, _, out_dim = weight.shape
        num_rels = w_comp.shape[0]
        V = weight.reshape(in_dim, num_bases, out_dim)
        W_rel = jnp.matmul(w_comp, V).reshape(num_rels, in_dim, out_dim)
        h_src = h[src]
        z_src = h_src @ Ws.T
        z_dst = h[dst] @ Ws.T
        z_e = he @ Ws.T
        e = jnp.concatenate([z_src, z_e, z_dst], axis=1) @ Wa.T
        msg = jnp.einsum('ei,eio->eo', h_src, W_rel[rel_type]) * e
        h_out = jax.ops.segment_sum(msg, dst, num_segments=n_nodes)
        return h_out

    def _L3_gnn_ref(x, edge_index, W, b):
        import jax, jax.numpy as jnp
        import numpy as np
        N_NODES = 125000
        n = x.shape[0]
        row, col = (edge_index[0], edge_index[1])
        h = x @ W
        deg = jax.ops.segment_sum(jnp.ones_like(col, dtype=h.dtype), col, num_segments=n) + 1.0
        dinv = jax.lax.rsqrt(deg)
        norm = dinv[row] * dinv[col]
        msgs = h[row] * norm[:, None]
        agg = jax.ops.segment_sum(msgs, col, num_segments=n)
        out = agg + h * (dinv * dinv)[:, None] + b
        return out
    edge_index = jnp.stack([src, dst])
    h = jnp.maximum(_layernorm(x, axis=-1), 0.0)
    x = x + _L0_gnn_ref(h, edge_index, L0_gnn_W1, L0_gnn_a_src1, L0_gnn_a_dst1, L0_gnn_b1, L0_gnn_W2, L0_gnn_a_src2, L0_gnn_a_dst2, L0_gnn_b2, L0_gnn_Wf, L0_gnn_bf)
    h = jnp.maximum(_layernorm(x, axis=-1), 0.0)
    x = x + _L1_gnn_ref(h, edge_index, edge_attr_16)
    h = jnp.maximum(_layernorm(x, axis=-1), 0.0)
    x = x + _L2_gnn_ref(h, edge_attr_16, L2_gnn_Ws, L2_gnn_Wa, L2_gnn_weight, L2_gnn_w_comp, src, dst, edge_type_90)
    h = jnp.maximum(_layernorm(x, axis=-1), 0.0)
    x = x + _L3_gnn_ref(h, edge_index, L3_gnn_W, L3_gnn_b)
    return x

_drawn_inputs = setup_inputs


def setup_inputs(seed=0):
    import zlib

    import numpy as np

    out = dict(_drawn_inputs(seed))
    spreads = {'L0_gnn_b1': (0.0, 0.1),
     'L0_gnn_b2': (0.0, 0.1),
     'L0_gnn_bf': (0.0, 0.1),
     'L3_gnn_b': (0.0, 0.1)}
    factors = {'L0_gnn_a_src1': 24.78,
     'L0_gnn_a_dst1': 193.435,
     'L0_gnn_a_src2': 171.046,
     'L0_gnn_a_dst2': 200.0}
    for name, (base, spread) in spreads.items():
        noise = np.random.default_rng([zlib.crc32(name.encode()), seed]).standard_normal(out[name].shape)
        drawn = base * np.exp(spread * noise) if base else spread * noise
        out[name] = jnp.asarray(drawn.astype(out[name].dtype))
    for name, factor in factors.items():
        out[name] = (out[name] * factor).astype(out[name].dtype)
    return out
```

```python
from contextlib import ExitStack

import concourse.bass as bass
from concourse import mybir

ALU = mybir.AluOpType
ACT = mybir.ActivationFunctionType
AX_X = mybir.AxisListType.X
F32 = mybir.dt.float32
BF16 = mybir.dt.bfloat16
I32 = mybir.dt.int32
RMAX = bass.bass_isa.ReduceOp.max

P = 128
T = 52
TB = 7
TH = 26
FEAT = 16
SLOPE = 0.2
BIG = 1.0e30
SKIP = float(1 << 23)
RNE = 12582912.0
LAM = 1.0507009873554805
LAMALPHA = LAM * 1.6732632423543772


class Layer:

    def __init__(self, name, heads, feat, table, width, has_dst):
        self.name, self.H, self.D, self.table, self.W, self.has_dst = name, heads, feat, table, width, has_dst


def gnn_kernel(nc, x, src, dst, edge_attr, edge_type, W1, a_src1, a_dst1, b1, W2, a_src2, a_dst2, b2,
               Wf, bf, Ws, Wa, weight, w_comp, W3, b3, out):
    N, _ = x.shape
    E, = src.shape
    K = -(-N // P)
    NP = P * K
    C = -(-E // (P * 2 * T)) * 2 * T
    EP = P * C
    NCH = C // T
    NTB = K // TB
    NPAIR = K // 2
    H1, C1 = a_src1.shape
    C2 = a_src2.shape[1]
    HC1 = H1 * C1
    R, B = w_comp.shape
    G4 = T // 4
    M2 = FEAT * FEAT
    ELAST = E - (P - 1) * C
    NLAST = N - (P - 1) * K
    assert K % (2 * TB) == 0 and NCH % 2 == 0 and T % 4 == 0 and C % (2 * TH) == 0 and 0 < ELAST <= C
    AH = H1 * FEAT
    L1 = Layer("gat1", H1, FEAT, FEAT + H1, 2 * H1 + AH + FEAT, True)
    L2 = Layer("gat2", 1, C2, C2 + 1, 2 + C2, True)
    L3 = Layer("rel", 1, FEAT, FEAT + 1, FEAT, True)
    L4 = Layer("gcn", 1, FEAT, FEAT, FEAT, False)
    LAYERS = [L1, L2, L3, L4]
    WMAX = L1.W

    with ExitStack() as ctx:
        def sb(name, shape, dt=F32):
            return ctx.enter_context(nc.sbuf_tensor(name, shape, dt))

        def sem(name):
            return ctx.enter_context(nc.semaphore(name))

        def dram(name, shape, dt=F32):
            return nc.dram_tensor(name, shape, dt, kind="Internal").ap()

        e_src, e_dst, e_typ = (dram(f"e_{n}", [EP, 1], I32) for n in ("src", "dst", "typ"))
        e_attr = dram("e_attr", [EP, FEAT])
        next_slot = dram("next_slot", [NP, 1])
        rowend_d = dram("rowend_d", [NP, 1])
        dlast_d = dram("dlast_d", [P, 1])
        wrel_d = dram("wrel_d", [FEAT * R, FEAT])
        for L in LAYERS:
            L.tab = dram(f"tab_{L.name}", [NP, L.table])
            L.scan = dram(f"scan_{L.name}", [EP, L.W])
            L.last_d = dram(f"last_{L.name}", [P, L.W])
            if L.has_dst:
                L.dnode = dram(f"dnode_{L.name}", [NP, L.H])
                L.dput = dram(f"dput_{L.name}", [EP, L.H])

        notb = sb("notb", [P, C])
        dst_f = sb("dst_f", [P, C])
        tE = sb("tE", [P, C])
        dst_i = tE[:, :].bitcast(I32)
        arena = sb("arena", [P, P * WMAX])
        scanbuf = sb("scanbuf", [P, 2 * T * WMAX])
        gbuf = sb("gbuf", [P, 2 * T * L2.table])
        idx = sb("idx", [P, 2, T], I32)
        dput = sb("dput", [P, 2, T * H1])
        attr = sb("attr", [P, 2, T * FEAT])
        typ = sb("typ", [P, 2, T], I32)
        ph = sb("ph", [P, T, AH])
        dsc = sb("dsc", [P, 2, T * H1])
        lgt = sb("lgt", [P, 2, T * H1])
        ex = sb("ex", [P, 2, T * H1])
        emax = sb("emax", [P, (T + 1) * H1])
        nb = sb("nb", [P, T])
        negb = sb("negb", [P, T])
        iq_i = sb("iq_i", [P, P], I32)
        ip_i = sb("ip_i", [P, 1], I32)
        iq = sb("iq", [P, P])
        ip = sb("ip", [P, 1])
        iqb = sb("iqb", [P, P], BF16)
        ident = sb("ident", [P, P])
        lower = sb("lower", [P, P])
        mask = sb("mask", [P, P])
        negmask = sb("negmask", [P, P])
        sq1 = sb("sq1", [P, P])
        sq2 = sb("sq2", [P, P])
        hd = sb("hd", [P, 4, TH])
        cnt = sb("cnt", [P, K])
        has = sb("has", [P, K])
        re = sb("re", [P, K])
        rs = sb("rs", [P, K])
        nt = sb("nt", [P, 2, K])
        rs_idx = sb("rs_idx", [P, K], I32)
        re_idx = sb("re_idx", [P, K], I32)
        nidx = sb("nidx", [P, 2, TB], I32)
        nval = sb("nval", [P, 2, TB * H1])
        nrow = sb("nrow", [P, 2, TB * WMAX])
        flag = sb("flag", [P, 4])
        flag_i = sb("flag_i", [P, 1], I32)
        nxt = sb("nxt", [P, 1], I32)
        dfirst_i = sb("dfirst_i", [P, 1], I32)
        fix_i = sb("fix_i", [P, 1], I32)
        col = sb("col", [P, 16])
        xs = sb("xs", [P, K * FEAT])
        hs = sb("hs", [P, K * FEAT])
        tab = sb("tab", [P, K * (C2 + 2)])
        snode = sb("snode", [P, K * H1])
        dnode = sb("dnode", [P, K * H1])
        nex = sb("nex", [P, 2 * K * H1])
        nm = sb("nm", [P, 2 * K * H1])
        dfv = sb("dfv", [P, H1])
        frow = sb("frow", [P, WMAX])
        crow = sb("crow", [P, WMAX])
        fx = sb("fx", [P, 8 * H1])
        W1b = scanbuf[:, 0:FEAT * HC1]
        as1 = sb("as1", [P, 2, HC1])
        ws1 = sb("ws1", [P, 2, AH])
        W1bd = sb("W1bd", [AH, HC1])
        b1c = sb("b1c", [HC1, 2])
        W2e = sb("W2e", [HC1, C2 + 2])
        as2 = sb("as2", [HC1, 2, C2])
        t2 = sb("t2", [HC1, 2, C2])
        b2b = sb("b2b", [P, C2])
        Wf_s = sb("Wf_s", [C2, FEAT])
        bfb = sb("bfb", [P, FEAT])
        Wsb = sb("Wsb", [P, M2])
        Wab = sb("Wab", [P, 3 * FEAT])
        wv = sb("wv", [P, 3, FEAT])
        wvt = sb("wvt", [P, M2])
        wct = sb("wct", [B, R])
        Vs = sb("Vs", [B, FEAT * FEAT])
        wm = sb("wm", [P, M2])
        wr = sb("wr", [P, 2, M2])
        wsp = sb("wsp", [P, 3, M2], BF16)
        W3s = sb("W3s", [FEAT, FEAT])
        b3b = sb("b3b", [P, FEAT])
        stg = sb("stg", [P, 2 * AH])
        aT = sb("aT", [P, 2 * P])
        hT = sb("hT", [P, 2, 2 * P])
        typ_f = sb("typ_f", [P, T])
        typT = sb("typT", [T, P], BF16)
        oh = sb("oh", [P, 2, 4 * P], BF16)
        prod = sb("prod", [P, 4 * M2])
        ef = sb("ef", [P, T])
        sel = scanbuf[:, 2 * T * L2.W:2 * T * L2.W + T * P // 2].bitcast(BF16)
        oneA = scanbuf[:, 0:TH * P].bitcast(BF16)
        oneB = scanbuf[:, TH * P:TH * P + TH * K].bitcast(BF16)

        ps = ctx.enter_context(nc.psum_tensor("ps", [P, 8, 512], F32))

        s_iota, s_pad, s_v = sem("s_iota"), sem("s_pad"), sem("s_v")
        s_dst_in, s_x, s_w = sem("s_dst_in"), sem("s_x"), sem("s_w")
        s_zero, s_zfill, s_viol, s_allred, s_tail = (sem(n) for n in ("s_zero", "s_zfill", "s_viol", "s_allred", "s_tail"))
        s_onehot, s_hist = sem("s_onehot"), sem("s_hist")
        s_rows, s_rowsst, s_copy, s_edges, s_dstre = (sem(n) for n in ("s_rows", "s_rowsst", "s_copy", "s_edges", "s_dstre"))
        s_dends, s_dlb, s_ref = (sem(n) for n in ("s_dends", "s_dlb", "s_ref"))
        s_wm, s_wmc, s_wrl = (sem(n) for n in ("s_wm", "s_wmc", "s_wrl"))
        s_fin, s_out = sem("s_fin"), sem("s_out")
        s_exq, s_exd = sem("s_exq"), sem("s_exd")
        for L in LAYERS:
            n = L.name
            L.s_tab, L.s_tabst, L.s_chain, L.s_rows = (sem(f"{q}_{n}") for q in ("tab", "tabst", "chain", "rows"))
            L.s_idx = [sem(f"idx{b}_{n}") for b in range(2)]
            L.s_g = [sem(f"g{b}_{n}") for b in range(2)]
            L.s_st = [sem(f"st{b}_{n}") for b in range(2)]
            L.s_last, L.s_fr, L.s_mend = (sem(f"{q}_{n}") for q in ("last", "fr", "mend"))
            L.s_ni, L.s_nf = sem(f"ni_{n}"), sem(f"nf_{n}")
            L.s_ng = [sem(f"ng{b}_{n}") for b in range(2)]
            if L.has_dst:
                L.s_stage, L.s_df, L.s_dput = sem(f"stage_{n}"), sem(f"df_{n}"), sem(f"dput_{n}")
                L.s_scat = [sem(f"scat{b}_{n}") for b in range(2)]
                L.s_in = [sem(f"in{b}_{n}") for b in range(2)]
            if L is L1 or L is L2:
                L.s_e, L.s_ed = sem(f"e_{n}"), sem(f"ed_{n}")
        s_lt, mlp_out = sem("sort_lt"), sem("mlp_out")
        s_mpe, s_mc, s_ma, s_ms = (sem(n) for n in ("mlp_pe", "mlp_c", "mlp_a", "mlp_s"))
        lin = {n: [sem(f"{n}_{q}") for q in ("pe", "c", "f")] for n in ("head", "gcnw")}
        s_ready = sem("ready")
        s_past, s_pe_past = sem("pool_past"), sem("pe_past")
        s_tyf, s_tyt, s_tyc, s_B, s_oh, s_Wr, s_wfree = (sem(n) for n in ("tyf", "tyt", "tyc", "rel_B", "rel_oh", "rel_W", "rel_free"))

        def edges(a):
            return a.rearrange("(p c) f -> p (c f)", p=P)

        def nodes(a):
            return a.rearrange("(p k) f -> p (k f)", p=P)

        xs3 = xs[:, :].rearrange("p (k i) -> p k i", i=FEAT)
        hs3 = hs[:, :].rearrange("p (k i) -> p k i", i=FEAT)

        def rows_of(L):
            return scanbuf[:, 0:2 * T * L.W].rearrange("p (b t f) -> p b t f", b=2, t=T)

        def gath(L):
            return gbuf[:, 0:2 * T * L.table].rearrange("p (b t f) -> p b t f", b=2, t=T)

        def last_rows(L):
            return arena[:, 0:P * L.W].rearrange("p (q f) -> p q f", q=P)

        def node_rows(L):
            return arena[:, 0:K * L.W].rearrange("p (k f) -> p k f", k=K)

        def tab3(w):
            return tab[:, 0:K * w].rearrange("p (k f) -> p k f", k=K)

        def kh(a, h):
            return a[:, 0:K * h].rearrange("p (k h) -> p k h", h=h)

        def bc(a, shape):
            return a.to_broadcast(shape)

        sort_sems = [sem(f"sort{n}") for n in range(12)]
        so_i = sb("so_i", [P, 4], I32)
        so_row = sb("so_row", [P, P], I32)
        so_attr = sb("so_attr", [P, FEAT])
        so_f = sb("so_f", [P, 8])
        so_eq = sb("so_eq", [P, 2, P])
        so_lt = sb("so_lt", [P, P])
        so_pos = sb("so_pos", [P, 2], I32)

        def sort_edges(pool):
            s_ld = sort_sems[0:5]
            s_cnt, s_op, s_cn = sort_sems[5:8]
            s_sc = sort_sems[8:12]
            g = nc.gpsimd
            pool.wait_ge(s_rowsst, 32)
            full = E // P
            OPS = 14

            def tile(i, n):
                e0 = i * P
                part = lambda a: a[bass.ds(e0, n)].rearrange("(p o) -> p o", o=1)
                pool.dma_start(so_i[0:n, 0:1], part(dst)).then_inc(s_ld[0], 16)
                pool.dma_start(so_i[0:n, 1:2], part(src)).then_inc(s_ld[1], 16)
                pool.dma_start(so_i[0:n, 2:3], part(edge_type)).then_inc(s_ld[2], 16)
                pool.dma_start(so_attr[0:n, :], edge_attr[bass.ds(e0, n), :]).then_inc(s_ld[3], 16)
                pool.dma_start(so_row[0:n, 0:n], dst[bass.ds(e0, n)].partition_broadcast(n)).then_inc(s_ld[4], 16)
                for s in s_ld:
                    pool.wait_ge(s, (i + 1) * 16)
                pool.sem_inc(s_past, 1)
                pool.indirect_dma_start(out=so_f[0:n, 0:1], out_offset=None, in_=next_slot,
                                        in_offset=bass.IndirectOffsetOnAxis(ap=so_i[0:n, 0:1], axis=0)).then_inc(s_cnt, 16)
                ops = [0]

                def chain(ins):
                    ops[0] += 1
                    ins.then_inc(s_op, 1)
                    pool.wait_ge(s_op, i * OPS + ops[0])

                f = lambda c: so_f[0:n, c:c + 1]
                g.tensor_copy(f(1), so_i[0:n, 0:1])
                chain(g.tensor_copy(so_eq[0:n, 0, 0:n], so_row[0:n, 0:n]))
                pool.sem_inc(s_past, 1)
                chain(g.tensor_scalar(so_eq[0:n, 1, 0:n], so_eq[0:n, 0, 0:n], f(1), None, ALU.is_equal))
                chain(g.tensor_tensor(so_eq[0:n, 0, 0:n], so_eq[0:n, 1, 0:n], so_lt[0:n, 0:n], ALU.mult))
                w = P
                while w > 1:
                    w //= 2
                    chain(g.tensor_tensor(so_eq[0:n, :, 0:w], so_eq[0:n, :, 0:w], so_eq[0:n, :, w:2 * w], ALU.add))
                pool.wait_ge(s_cnt, (i + 1) * 16)
                g.tensor_tensor(f(2), f(0), so_eq[0:n, 0, 0:1], ALU.add)
                g.tensor_tensor(f(3), f(0), so_eq[0:n, 1, 0:1], ALU.add)
                chain(g.tensor_tensor(f(4), so_eq[0:n, 1, 0:1], so_eq[0:n, 0, 0:1], ALU.subtract))
                pool.sem_inc(s_past, 1)
                g.tensor_copy(so_pos[0:n, 0:1], f(2))
                chain(g.tensor_scalar(f(5), f(4), SKIP, -SKIP, ALU.mult, ALU.add))
                chain(g.tensor_tensor(f(6), f(5), f(1), ALU.add))
                pool.sem_inc(s_past, 1)
                chain(g.tensor_copy(so_pos[0:n, 1:2], f(6)))
                assert ops[0] == OPS
                pool.sem_inc(s_past, 1)
                pool.indirect_dma_start(out=next_slot, out_offset=bass.IndirectOffsetOnAxis(ap=so_pos[0:n, 1:2], axis=0),
                                        in_=f(3), in_offset=None, bounds_check=NP - 1, oob_is_err=False).then_inc(s_cn, 16)
                for q, (o, a) in enumerate(((e_dst, so_i[0:n, 0:1]), (e_src, so_i[0:n, 1:2]), (e_typ, so_i[0:n, 2:3]),
                                            (e_attr, so_attr[0:n, :]))):
                    pool.indirect_dma_start(out=o, out_offset=bass.IndirectOffsetOnAxis(ap=so_pos[0:n, 0:1], axis=0),
                                            in_=a, in_offset=None).then_inc(s_sc[q], 16)
                for s in (s_cn, *s_sc):
                    pool.wait_ge(s, (i + 1) * 16)
                pool.sem_inc(s_past, 1)

            g.memset(so_lt[:, :], 1.0).then_inc(s_lt, 1)
            pool.wait_ge(s_lt, 1)
            g.affine_select(out=so_lt[:, :], in_=so_lt[:, :], compare_op=ALU.is_gt, fill=0.0, base=0,
                            pattern=[[-1, P]], channel_multiplier=1).then_inc(s_lt, 1)
            pool.wait_ge(s_lt, 2)
            g.memset(so_eq[:, :, :], 0.0).then_inc(s_lt, 1)
            pool.wait_ge(s_lt, 3)
            with pool.Fori(0, full) as i:
                tile(i, P)
            if E % P:
                g.memset(so_eq[:, :, :], 0.0).then_inc(s_lt, 1)
                pool.wait_ge(s_lt, 4)
                tile(full, E % P)

        block = ctx.enter_context(nc.Block())

        @block.sync
        def _(sp):
            sp.wait_ge(s_pad, 1)
            sp.dma_start(dst_i[0:P - 1, :], dst[0:(P - 1) * C].rearrange("(p c) -> p c", c=C)).then_inc(s_dst_in, 16)
            sp.dma_start(dst_i[P - 1:P, 0:ELAST], dst[(P - 1) * C:E].rearrange("(o c) -> o c", o=1)).then_inc(s_dst_in, 16)
            sp.dma_start(nxt[0:P - 1, :], dst[C:(P - 1) * C + 1:C].rearrange("(p o) -> p o", o=1),
                         allow_slow_non_contiguous=True).then_inc(s_dst_in, 16)
            sp.dma_start(xs[0:P - 1, :], x[0:(P - 1) * K, :].rearrange("(p k) i -> p (k i)", k=K)).then_inc(s_x, 16)
            sp.dma_start(xs[P - 1:P, 0:NLAST * FEAT], x[(P - 1) * K:N, :].rearrange("(o k) i -> o (k i)", o=1)).then_inc(s_x, 16)
            for o, i in (
                (as1[:, 0, :], a_src1.rearrange("h c -> (h c)").partition_broadcast(P)),
                (as1[:, 1, :], a_dst1.rearrange("h c -> (h c)").partition_broadcast(P)),
                (b1c[:, 0:1], b1.rearrange("(c o) -> c o", o=1)),
                (W2e[:, 0:C2], W2),
                (as2[:, 0, :], a_src2.rearrange("h c -> (h c)").partition_broadcast(HC1)),
                (as2[:, 1, :], a_dst2.rearrange("h c -> (h c)").partition_broadcast(HC1)),
                (b2b[:, :], b2.partition_broadcast(P)),
                (Wf_s[:, :], Wf),
                (bfb[:, :], bf.partition_broadcast(P)),
                (Wsb[:, :], Ws.rearrange("o i -> (o i)").partition_broadcast(P)),
                (Wab[:, :], Wa.rearrange("o i -> (o i)").partition_broadcast(P)),
                (Vs[:, :].rearrange("b (a o) -> b a o", a=FEAT),
                 weight.rearrange("b i o -> (b i o)").rearrange("(a b o) -> b a o", a=FEAT, b=B)),
                (W3s[:, :], W3),
                (b3b[:, :], b3.partition_broadcast(P)),
            ):
                sp.dma_start(o, i).then_inc(s_w, 16)
            sp.dma_start(wct[:, :], w_comp.rearrange("r b -> b r"), allow_slow_non_contiguous=True).then_inc(s_w, 16)
            for h in range(H1):
                sp.dma_start(W1bd[h * FEAT:(h + 1) * FEAT, h * C1:(h + 1) * C1],
                             W1[:, h * C1:(h + 1) * C1]).then_inc(s_w, 16)
            sp.dma_start(W1b, W1.rearrange("i c -> (i c)").partition_broadcast(P)).then_inc(s_w, 16)
            sp.wait_ge(s_zero, 1)
            sp.wait_ge(s_dst_in, 48)
            zrow = arena[0:1, 0:(EP - E) * FEAT]
            sp.dma_start(e_src[E:EP, :].rearrange("e o -> o e"), zrow[:, 0:EP - E].bitcast(I32)).then_inc(s_tail, 16)
            sp.dma_start(e_typ[E:EP, :].rearrange("e o -> o e"), zrow[:, 0:EP - E].bitcast(I32)).then_inc(s_tail, 16)
            sp.dma_start(e_attr[E:EP, :].rearrange("(o e) f -> o (e f)", o=1), zrow).then_inc(s_tail, 16)
            sp.dma_start(e_dst[E:EP, :].rearrange("e o -> o e"), dst_i[P - 1:P, ELAST:C]).then_inc(s_tail, 16)
            for L in LAYERS:
                if L.has_dst:
                    for h in range(L.H):
                        sp.dma_start(edges(L.dput)[:, h * C:(h + 1) * C], arena[:, 0:C]).then_inc(s_zfill, 16)
            sp.wait_ge(s_wmc, 1)
            sp.wait_ge(s_zero, 2)
            sp.dma_start(wrel_d.rearrange("(a r) o -> r a o", a=FEAT),
                         wm[0:R, :].rearrange("r (a o) -> r a o", a=FEAT)).then_inc(s_wrl, 16)
            sp.wait_ge(s_wrl, 16)
            sp.dma_start(wr[0:R, 0, :], wrel_d.rearrange("(r i) o -> r (i o)", i=FEAT)).then_inc(s_wrl, 16)
            sp.wait_ge(s_rows, 1)
            sp.dma_start(nodes(rowend_d), re[:, :]).then_inc(s_rowsst, 16)
            sp.dma_start(nodes(next_slot), rs[:, :]).then_inc(s_rowsst, 16)
            sp.wait_ge(s_edges, 1)
            sp.dma_start(dst_i, edges(e_dst)).then_inc(s_dstre, 16)
            sp.wait_ge(s_dends, 2)
            sp.dma_start(dlast_d, col[:, 1:2]).then_inc(s_dlb, 16)
            sp.wait_ge(s_dlb, 16)
            sp.dma_start(sq1[:, :], dlast_d.rearrange("q o -> (q o)").partition_broadcast(P)).then_inc(s_dlb, 16)

            def layer(L):
                sp.wait_ge(L.s_tab, 1)
                sp.dma_start(nodes(L.tab), tab[:, 0:K * L.table]).then_inc(L.s_tabst, 16)
                if L.has_dst:
                    sp.dma_start(nodes(L.dnode), dnode[:, 0:K * L.H]).then_inc(L.s_tabst, 16)
                    sp.wait_ge(L.s_df, 16)
                    for b in range(2):
                        sp.wait_ge(L.s_scat[b], 16 * TB * (NTB // 2))
                    sp.dma_start(edges(L.dput)[:, 0:L.H], dfv[:, 0:L.H], allow_slow_non_contiguous=True).then_inc(L.s_dput, 16)
                    sp.wait_ge(L.s_dput, 16)
                with sp.Fori(0, NCH // 2) as i:
                    for b in range(2):
                        sp.wait_ge(L.s_rows, i * 2 + (b + 1))
                        sp.dma_start(idx[:, b, :], edges(e_src)[:, bass.ds((i * 2 + b) * T, T)]).then_inc(L.s_idx[b], 16)
                        if L.has_dst:
                            sp.dma_start(dput[:, b, 0:T * L.H], edges(L.dput)[:, bass.ds((i * 2 + b) * (T * L.H), T * L.H)])\
                              .then_inc(L.s_in[b], 16)
                        if L is L1:
                            sp.dma_start(attr[:, b, :], edges(e_attr)[:, bass.ds((i * 2 + b) * (T * FEAT), T * FEAT)])\
                              .then_inc(L.s_in[b], 16)
                        if L is L3:
                            sp.dma_start(typ[:, b, :], edges(e_typ)[:, bass.ds((i * 2 + b) * T, T)]).then_inc(L.s_in[b], 16)
                sp.wait_ge(L.s_rows, NCH + 2)
                sp.dma_start(L.last_d, rows_of(L)[:, 1, T - 1, :]).then_inc(L.s_last, 16)
                sp.wait_ge(L.s_last, 16)
                sp.dma_start(arena[:, 0:P * L.W], L.last_d.rearrange("q f -> (q f)").partition_broadcast(P)).then_inc(L.s_last, 16)

            for L in LAYERS:
                layer(L)
            sp.wait_ge(s_fin, 1)
            sp.dma_start(out[0:(P - 1) * K, :].rearrange("(p k) i -> p (k i)", k=K), xs[0:P - 1, :]).then_inc(s_out, 16)
            sp.dma_start(out[(P - 1) * K:N, :].rearrange("(o k) i -> o (k i)", o=1), xs[P - 1:P, 0:NLAST * FEAT]).then_inc(s_out, 16)
            sp.wait_ge(s_out, 32)

        @block.gpsimd
        def _(pool):
            nc.gpsimd.iota(iq_i[:, :], [[1, P]], base=0, channel_multiplier=0).then_inc(s_iota, 1)
            nc.gpsimd.iota(ip_i[:, :], [[0, 1]], base=0, channel_multiplier=1).then_inc(s_iota, 1)
            pool.wait_ge(s_viol, 1)
            nc.gpsimd.partition_all_reduce(flag[:, 1:2], flag[:, 0:1], P, RMAX).then_inc(s_allred, 1)
            pool.wait_ge(s_allred, 1)
            nc.gpsimd.tensor_copy(flag_i[:, :], flag[:, 1:2]).then_inc(s_allred, 1)
            pool.wait_ge(s_allred, 2)
            unsorted = pool.value_load(flag_i[0:1, 0:1], min_val=0, max_val=1)
            with pool.If(unsorted):
                sort_edges(pool)
            with pool.Else():
                pool.dma_start(e_src[0:E, :], src.rearrange("(e o) -> e o", o=1)).then_inc(s_copy, 16)
                pool.dma_start(e_dst[0:E, :], dst.rearrange("(e o) -> e o", o=1)).then_inc(s_copy, 16)
                pool.dma_start(e_typ[0:E, :], edge_type.rearrange("(e o) -> e o", o=1)).then_inc(s_copy, 16)
                pool.dma_start(e_attr[0:E, :], edge_attr).then_inc(s_copy, 16)
                pool.wait_ge(s_copy, 64)
            pool.wait_ge(s_tail, 64)
            pool.sem_inc(s_edges, 1)

            pool.wait_ge(s_dends, 1)
            pool.wait_ge(s_rowsst, 32)
            pool.indirect_dma_start(out=col[:, 2:3], out_offset=None, in_=rowend_d,
                                    in_offset=bass.IndirectOffsetOnAxis(ap=dfirst_i[:, :], axis=0)).then_inc(s_ref, 16)
            pool.wait_ge(s_zfill, 16 * sum(L.H for L in LAYERS if L.has_dst))

            def layer(L):
                NTAB = 32 if L.has_dst else 16
                pool.wait_ge(L.s_tabst, NTAB)
                if L.has_dst:
                    pool.indirect_dma_start(out=dfv[:, 0:L.H], out_offset=None, in_=L.dnode,
                                            in_offset=bass.IndirectOffsetOnAxis(ap=dfirst_i[:, :], axis=0)).then_inc(L.s_df, 16)
                    with pool.Fori(0, NTB // 2) as i:
                        for b in range(2):
                            pool.wait_ge(L.s_stage, i * 2 + (b + 1))
                            pool.sem_inc(s_past, 1)
                            for t in range(TB):
                                pool.indirect_dma_start(
                                    out=L.dput, out_offset=bass.IndirectOffsetOnAxis(ap=nidx[:, b, t:t + 1], axis=0),
                                    in_=nval[:, b, t * L.H:(t + 1) * L.H], in_offset=None,
                                    bounds_check=EP - 1, oob_is_err=False).then_inc(L.s_scat[b], 16)
                with pool.Fori(0, NCH // 2) as i:
                    for b in range(2):
                        pool.wait_ge(L.s_idx[b], (i + 1) * 16)
                        pool.sem_inc(s_past, 1)
                        for t in range(T):
                            pool.indirect_dma_start(
                                out=gath(L)[:, b, t, :], out_offset=None, in_=L.tab,
                                in_offset=bass.IndirectOffsetOnAxis(ap=idx[:, b, t:t + 1], axis=0)).then_inc(L.s_g[b], 16)
                for b in range(2):
                    pool.wait_ge(L.s_st[b], 16 * (NCH // 2 + 1))
                pool.indirect_dma_start(out=frow[:, 0:L.W], out_offset=None, in_=L.scan,
                                        in_offset=bass.IndirectOffsetOnAxis(ap=fix_i[:, :], axis=0),
                                        bounds_check=EP - 1, oob_is_err=False).then_inc(L.s_fr, 16)
                pool.wait_ge(L.s_mend, 1)
                pool.indirect_dma_start(out=L.scan, out_offset=bass.IndirectOffsetOnAxis(ap=fix_i[:, :], axis=0),
                                        in_=frow[:, 0:L.W], in_offset=None,
                                        bounds_check=EP - 1, oob_is_err=False).then_inc(L.s_fr, 16)
                pool.wait_ge(L.s_fr, 32)
                with pool.Fori(0, NTB // 2) as i:
                    for b in range(2):
                        pool.wait_ge(L.s_ni, i * 2 + (b + 1))
                        pool.wait_ge(L.s_nf, i * 2 + (b + 1))
                        pool.sem_inc(s_past, 1)
                        for t in range(TB):
                            pool.indirect_dma_start(
                                out=nrow[:, b, t * L.W:(t + 1) * L.W], out_offset=None, in_=L.scan,
                                in_offset=bass.IndirectOffsetOnAxis(ap=nidx[:, b, t:t + 1], axis=0)).then_inc(L.s_ng[b], 16)

            for L in LAYERS:
                layer(L)

        @block.scalar
        def _(act):
            act.wait_ge(s_wm, 1)
            nc.scalar.copy(wm[0:R, :], ps[0:R, 3, 0:M2]).then_inc(s_wmc, 1)

            asked = [0]

            def answer(a, func=ACT.Exp):
                asked[0] += 1
                act.wait_ge(s_exq, asked[0])
                nc.scalar.activation(a, a, func).then_inc(s_exd, 1)

            def edge_loop(L):
                for b in range(2):
                    act.wait_ge(L.s_rows, 2)
                    act.dma_start(edges(L.scan)[:, b * T * L.W:(b + 1) * T * L.W],
                                  rows_of(L)[:, b, :, :].rearrange("p t f -> p (t f)")).then_inc(L.s_st[b], 16)
                with act.Fori(0, NCH // 2) as i:
                    for b in range(2):
                        if L is L1 or L is L2:
                            act.wait_ge(L.s_e, i * 2 + (b + 1))
                            nc.scalar.activation(ex[:, :, 0:T * L.H], ex[:, :, 0:T * L.H], ACT.Exp).then_inc(L.s_ed, 1)
                        if L is L3:
                            act.wait_ge(L.s_in[b], (i + 1) * 32)
                            nc.scalar.copy(typ_f[:, :], typ[:, b, :]).then_inc(s_tyf, 1)
                            act.wait_ge(s_tyt, i * 2 + (b + 1))
                            nc.scalar.copy(typT[:, :], ps[0:T, 2, 0:P]).then_inc(s_tyc, 1)
                        act.wait_ge(L.s_rows, i * 2 + (b + 3))
                        act.dma_start(edges(L.scan)[:, bass.ds((i * 2 + b) * (T * L.W), T * L.W)],
                                      rows_of(L)[:, b, :, :].rearrange("p t f -> p (t f)")).then_inc(L.s_st[b], 16)

            def node_indices(L):
                act.wait_ge(L.s_fr, 32)
                for b in range(2):
                    nc.scalar.copy(nidx[:, b, :], re_idx[:, b * TB:(b + 1) * TB]).then_inc(L.s_ni, 1)
                with act.Fori(1, NTB // 2) as i:
                    for b in range(2):
                        act.wait_ge(L.s_ng[b], i * (16 * TB))
                        nc.scalar.copy(nidx[:, b, :], re_idx[:, bass.ds((i * 2 + b) * TB, TB)]).then_inc(L.s_ni, 1)

            def linear(s, width):
                with act.Fori(0, NPAIR) as i:
                    act.wait_ge(s[0], i * 2 + 1)
                    nc.scalar.copy(aT[0:width, :], ps[0:width, 1, 0:2 * P]).then_inc(s[1], 1)

            def mend(L):
                for _ in range(L.H):
                    answer(sq2[:, :])
                answer(fx[:, 0:2 * L.H])

            answer(nt[:, 0, :], ACT.Sqrt)
            edge_loop(L1)
            mend(L1)
            node_indices(L1)
            answer(nex[:, 0:2 * K * H1])
            with act.Fori(0, NPAIR) as i:
                act.wait_ge(s_mpe, i * 3 + 1)
                nc.scalar.copy(aT[0:AH, :], ps[0:AH, 1, 0:2 * P]).then_inc(s_mc, 1)
                act.wait_ge(s_mpe, i * 3 + 2)
                nc.scalar.activation(hT[0:HC1, 0, :], ps[0:HC1, 2, 0:2 * P], ACT.Exp, bias=b1c[:, 0:1])
                nc.scalar.activation(hT[0:HC1, 1, :], ps[0:HC1, 2, 0:2 * P], ACT.Relu, bias=b1c[:, 1:2],
                                     scale=LAM).then_inc(s_ma, 1)
            edge_loop(L2)
            mend(L2)
            node_indices(L2)
            answer(nex[:, 0:2 * K])
            answer(scanbuf[:, 0:K * C2])
            linear(lin["head"], C2)
            answer(nt[:, 0, :], ACT.Sqrt)
            edge_loop(L3)
            node_indices(L3)
            answer(nt[:, 0, :], ACT.Sqrt)
            answer(nt[:, 0, :], ACT.Sqrt)
            linear(lin["gcnw"], FEAT)
            edge_loop(L4)
            node_indices(L4)

        @block.tensor
        def _(pe):
            pe.wait_ge(s_w, 16 * (16 + H1))
            nc.tensor.matmul(ps[0:R, 3, 0:M2], wct[:, :], Vs[:, :], start=True, stop=True).then_inc(s_wm, 1)
            pe.wait_ge(s_zero, 1)
            for _ in range(2):
                nc.tensor.matmul(ps[:, 0, 0:K], arena[:, 0:P], arena[:, P:P + K], start=True, stop=False,
                                 skip_group_check=True).then_inc(s_hist, 1)
            oA = oneA.rearrange("p (b t q) -> p b t q", b=2, t=TH)
            oB = oneB.rearrange("p (b t k) -> p b t k", b=2, t=TH)
            with pe.Fori(0, C // TH // 2) as i:
                for b in range(2):
                    pe.wait_ge(s_onehot, i * 2 + (b + 1))
                    for t in range(TH):
                        mm = nc.tensor.matmul(ps[:, 0, 0:K], oA[:, b, t, :], oB[:, b, t, :], start=False, stop=False,
                                              skip_group_check=True)
                    mm.then_inc(s_hist, 1)
            pe.wait_ge(s_onehot, C // TH + 1)
            nc.tensor.matmul(ps[:, 1, 0:1], lower[:, :], col[:, 0:1], start=True, stop=True).then_inc(s_hist, 1)

            def turn_pair(width):
                for j in range(2):
                    mm = nc.tensor.transpose(ps[0:width, 1, j * P:(j + 1) * P], stg[:, j * width:(j + 1) * width], ident[:, :])
                return mm

            def linear(s, width, w):
                with pe.Fori(0, NPAIR) as i:
                    pe.wait_ge(s[2], i * 2 + 1)
                    turn_pair(width).then_inc(s[0], 1)
                    pe.wait_ge(s[1], i + 1)
                    for j in range(2):
                        mm = nc.tensor.matmul(ps[:, 3, j * FEAT:(j + 1) * FEAT], aT[0:width, j * P:(j + 1) * P], w,
                                              start=True, stop=True)
                    mm.then_inc(s[0], 1)

            with pe.Fori(0, NPAIR) as i:
                pe.wait_ge(s_ms, i * 2 + 1)
                pe.sem_inc(s_pe_past, 1)
                turn_pair(AH).then_inc(s_mpe, 1)
                pe.wait_ge(s_mc, i + 1)
                nc.tensor.matmul(ps[0:HC1, 2, 0:2 * P], W1bd[:, :], aT[0:AH, :], start=True, stop=True).then_inc(s_mpe, 1)
                pe.wait_ge(s_ms, i * 2 + 2)
                for j in range(2):
                    mm = nc.tensor.matmul(ps[:, 3, j * (C2 + 2):(j + 1) * (C2 + 2)], hT[0:HC1, 0, j * P:(j + 1) * P],
                                          W2e[:, :], start=True, stop=True)
                mm.then_inc(s_mpe, 1)
            linear(lin["head"], C2, Wf_s[:, :])

            sel3 = sel.rearrange("k (t r) -> k t r", t=T)

            def spread(g):
                for j in range(4):
                    mm = nc.tensor.matmul(ps[:, g % 2, j * P:(j + 1) * P], sel3[0:T, (g % G4) * 4 + j, :], typT[:, :],
                                          start=True, stop=True)
                mm.then_inc(s_B, 1)

            pe.wait_ge(s_ready, 1)
            with pe.Fori(0, NCH // 2) as i:
                for b in range(2):
                    pe.wait_ge(s_tyf, i * 2 + (b + 1))
                    pe.sem_inc(s_pe_past, 1)
                    nc.tensor.transpose(ps[0:T, 2, 0:P], typ_f[:, :], ident[:, :]).then_inc(s_tyt, 1)
                    pe.wait_ge(s_tyc, i * 2 + (b + 1))
                    spread(b * G4)
                    for g in range(b * G4, (b + 1) * G4):
                        if g + 1 < (b + 1) * G4:
                            spread(g + 1)
                        pe.wait_ge(s_oh, i * (2 * G4) + (g + 1))
                        pe.wait_ge(s_wfree, i * (2 * G4) + (g + 1))
                        for j in range(4):
                            for part in range(3):
                                mm = nc.tensor.matmul(
                                    ps[:, 4 + 2 * (g % 2) + j // 2, (j % 2) * M2:(j % 2 + 1) * M2],
                                    oh[:, g % 2, j * P:(j + 1) * P], wsp[:, part, :], start=(part == 0), stop=(part == 2))
                        mm.then_inc(s_Wr, 1)
            linear(lin["gcnw"], FEAT, W3s[:, :])

        @block.vector
        def _(dve):
            v = nc.vector
            count = [0, 0]

            def link(ins):
                count[0] += 1
                ins.then_inc(s_v, 1)
                dve.wait_ge(s_v, count[0])

            def ask(ins):
                count[1] += 1
                ins.then_inc(s_exq, 1)
                dve.wait_ge(s_exd, count[1])

            def leaky(o, a):
                return v.scalar_tensor_tensor(out=o, in0=a, scalar=SLOPE, in1=a, op0=ALU.mult, op1=ALU.max)

            v.memset(dst_i, N)
            v.memset(nxt[:, :], N)
            v.memset(xs[:, :], 0.0)
            v.memset(W1bd[:, :], 0.0).then_inc(s_pad, 1)
            v.memset(arena[:, :], 0.0).then_inc(s_zero, 1)
            for L in LAYERS:
                dve.sem_inc(L.s_nf, 2)
            dve.sem_inc(s_wfree, 2)
            v.memset(dsc[:, :, :], 0.0)
            v.memset(emax[:, :], 0.0)
            v.memset(frow[:, :], 0.0)
            v.memset(wr[:, :, :], 0.0).then_inc(s_zero, 1)
            dve.wait_ge(s_zero, 2)

            dve.wait_ge(s_iota, 2)
            v.tensor_copy(iq[:, :], iq_i[:, :])
            v.tensor_copy(iqb[:, :], iq_i[:, :])
            link(v.tensor_copy(ip[:, :], ip_i[:, :]))
            v.tensor_scalar(ident[:, :], iq[:, :], ip[:, 0:1], None, ALU.is_equal)
            v.tensor_scalar(lower[:, :], iq[:, :], ip[:, 0:1], None, ALU.is_gt)
            link(v.tensor_scalar(mask[:, :], iq[:, :], ip[:, 0:1], None, ALU.is_lt))

            dve.wait_ge(s_dst_in, 48)
            v.tensor_copy(col[:, 3:4], nxt[:, :])
            link(v.tensor_copy(dst_f[:, :], dst_i))
            v.tensor_tensor(notb[:, 1:C], dst_f[:, 0:C - 1], dst_f[:, 1:C], ALU.is_gt)
            link(v.tensor_tensor(notb[:, 0:1], dst_f[:, C - 1:C], col[:, 3:4], ALU.is_gt))
            v.tensor_reduce(flag[:, 0:1], notb[:, :], AX_X, ALU.max).then_inc(s_viol, 1)

            dve.wait_ge(s_w, 16 * (16 + H1))
            w1t = scanbuf[:, FEAT * HC1:2 * FEAT * HC1]
            for q in range(2):
                link(v.tensor_tensor(w1t.rearrange("p (i c) -> p i c", i=FEAT), W1b.rearrange("p (i c) -> p i c", i=FEAT),
                                     bc(as1[:, q, :].unsqueeze(1), [P, FEAT, HC1]), ALU.mult))
                link(v.tensor_reduce(ws1[:, q, :].rearrange("p (h i) -> p i h", h=H1),
                                     w1t.rearrange("p (i h c) -> p i h c", i=FEAT, h=H1), AX_X, ALU.add))
            v.tensor_scalar(b1c[:, 1:2], b1c[:, 0:1], LAM, None, ALU.mult)
            link(v.tensor_tensor(t2[:, :, :], bc(W2e[:, 0:C2].unsqueeze(1), [HC1, 2, C2]), as2[:, :, :], ALU.mult))
            link(v.tensor_reduce(W2e[:, C2:C2 + 2], t2[:, :, :], AX_X, ALU.add))
            for q in range(3):
                link(v.tensor_tensor(wvt[:, :].rearrange("p (o i) -> p o i", o=FEAT),
                                     Wsb[:, :].rearrange("p (o i) -> p o i", o=FEAT),
                                     bc(Wab[:, q * FEAT:(q + 1) * FEAT].unsqueeze(2), [P, FEAT, FEAT]), ALU.mult))
                link(v.tensor_reduce(wv[:, q, :], wvt[:, :].rearrange("p (o i) -> p i o", o=FEAT), AX_X, ALU.add))

            def layernorm_relu():
                link(v.tensor_reduce(nt[:, 1, :], xs3, AX_X, ALU.add))
                link(v.tensor_scalar(nt[:, 1, :], nt[:, 1, :], 1.0 / FEAT, None, ALU.mult))
                link(v.tensor_tensor(hs3, xs3, bc(nt[:, 1, :].unsqueeze(2), [P, K, FEAT]), ALU.subtract))
                link(v.tensor_tensor(tab3(FEAT), hs3, hs3, ALU.mult))
                link(v.tensor_reduce(nt[:, 0, :], tab3(FEAT), AX_X, ALU.add))
                ask(v.tensor_scalar(nt[:, 0, :], nt[:, 0, :], 1.0 / FEAT, 1e-5, ALU.mult, ALU.add))
                link(v.reciprocal(nt[:, 0, :], nt[:, 0, :]))
                link(v.tensor_tensor(hs3, hs3, bc(nt[:, 0, :].unsqueeze(2), [P, K, FEAT]), ALU.mult))
                link(v.tensor_scalar(hs[:, :], hs[:, :], 0.0, None, ALU.max))

            def project(o, w, heads):
                tmp = scanbuf[:, 0:K * heads * FEAT].rearrange("p (k h i) -> p k h i", k=K, h=heads)
                link(v.tensor_tensor(tmp, bc(hs3.unsqueeze(2), [P, K, heads, FEAT]),
                                     bc(w.rearrange("p (h i) -> p h i", h=heads).unsqueeze(1), [P, K, heads, FEAT]), ALU.mult))
                link(v.tensor_reduce(o, tmp, AX_X, ALU.add))

            dve.wait_ge(s_x, 32)
            layernorm_relu()
            project(kh(snode, H1), ws1[:, 0, :], H1)
            project(kh(dnode, H1), ws1[:, 1, :], H1)
            v.tensor_copy(tab3(L1.table)[:, :, 0:FEAT], hs3)
            v.tensor_copy(tab3(L1.table)[:, :, FEAT:], kh(snode, H1)).then_inc(L1.s_tab, 1)

            oA = oneA.rearrange("p (b t q) -> p b t q", b=2, t=TH)
            oB = oneB.rearrange("p (b t k) -> p b t k", b=2, t=TH)
            hs_ = sem("hist_chain")
            hist_steps = 4
            with dve.Fori(0, C // TH // 2) as i:
                for b in range(2):
                    base = i * (2 * hist_steps) + b * hist_steps
                    d = dst_f[:, bass.ds((i * 2 + b) * TH, TH)]
                    v.tensor_scalar(hd[:, 0, :], d, 1.0 / K, 0.5 / K - 0.5, ALU.mult, ALU.add).then_inc(hs_, 1)
                    dve.wait_ge(hs_, base + 1)
                    v.tensor_scalar(hd[:, 1, :], hd[:, 0, :], RNE, None, ALU.add).then_inc(hs_, 1)
                    dve.wait_ge(hs_, base + 2)
                    v.tensor_scalar(hd[:, 2, :], hd[:, 1, :], RNE, None, ALU.subtract).then_inc(hs_, 1)
                    dve.wait_ge(hs_, base + 3)
                    v.scalar_tensor_tensor(out=hd[:, 3, :], in0=hd[:, 2, :], scalar=-float(K), in1=d,
                                           op0=ALU.mult, op1=ALU.add).then_inc(hs_, 1)
                    dve.wait_ge(s_hist, i * 2 + (b + 1))
                    v.tensor_tensor(oA[:, b, :, :], bc(iqb[:, :].unsqueeze(1), [P, TH, P]),
                                    bc(hd[:, 2, :].unsqueeze(2), [P, TH, P]), ALU.is_equal)
                    dve.wait_ge(hs_, base + 4)
                    v.tensor_tensor(oB[:, b, :, :], bc(iqb[:, 0:K].unsqueeze(1), [P, TH, K]),
                                    bc(hd[:, 3, :].unsqueeze(2), [P, TH, K]), ALU.is_equal).then_inc(s_onehot, 1)
            dve.wait_ge(s_hist, C // TH + 2)

            v.memset(nt[:, 1, :], 1.0)
            link(v.tensor_copy(cnt[:, :], ps[:, 0, 0:K]))
            link(v.tensor_tensor_scan(re[:, :], nt[:, 1, :], cnt[:, :], 0.0, ALU.mult, ALU.add))
            v.tensor_copy(col[:, 0:1], re[:, K - 1:K]).then_inc(s_onehot, 1)
            dve.wait_ge(s_hist, C // TH + 3)
            link(v.tensor_scalar(re[:, :], re[:, :], ps[:, 1, 0:1], None, ALU.add))
            v.tensor_scalar(has[:, :], cnt[:, :], 1.0, None, ALU.min)
            link(v.tensor_tensor(rs[:, :], re[:, :], cnt[:, :], ALU.subtract))
            v.tensor_scalar(re_idx[:, :], re[:, :], -1.0, 0.0, ALU.add, ALU.max)
            link(v.tensor_scalar(nt[:, 0, :], has[:, :], -SKIP, SKIP, ALU.mult, ALU.add))
            v.tensor_tensor(rs_idx[:, :], nt[:, 0, :], rs[:, :], ALU.add).then_inc(s_rows, 1)

            dve.wait_ge(s_dstre, 16)
            link(v.tensor_copy(dst_f[:, :], dst_i))
            v.tensor_tensor(notb[:, 1:C], dst_f[:, 1:C], dst_f[:, 0:C - 1], ALU.is_equal)
            v.memset(notb[:, 0:1], 0.0)
            v.tensor_copy(dfirst_i[:, :], dst_i[:, 0:1]).then_inc(s_dends, 1)
            v.tensor_copy(col[:, 1:2], dst_f[:, C - 1:C]).then_inc(s_dends, 1)
            dve.wait_ge(s_dlb, 32)
            link(v.tensor_scalar(sq2[:, :], sq1[:, :], dst_f[:, 0:1], None, ALU.is_equal))
            link(v.tensor_tensor(mask[:, :], mask[:, :], sq2[:, :], ALU.mult))
            v.tensor_scalar(negmask[:, :], mask[:, :], 1.0, BIG, ALU.subtract, ALU.mult)
            link(v.tensor_reduce(col[:, 4:5], mask[:, :], AX_X, ALU.max))
            dve.wait_ge(s_ref, 16)
            link(v.tensor_scalar(col[:, 5:6], ip[:, :], float(C), float(C), ALU.mult, ALU.add))
            link(v.tensor_tensor(col[:, 6:7], col[:, 2:3], col[:, 5:6], ALU.is_le))
            link(v.tensor_tensor(col[:, 6:7], col[:, 6:7], col[:, 4:5], ALU.mult))
            link(v.tensor_scalar(col[:, 6:7], col[:, 6:7], -SKIP, SKIP - 1.0, ALU.mult, ALU.add))
            link(v.tensor_tensor(fix_i[:, :], col[:, 2:3], col[:, 6:7], ALU.add))

            def stage_dst(L):
                w = TB * L.H
                for b in range(2):
                    v.tensor_copy(nval[:, b, 0:w], dnode[:, b * w:(b + 1) * w])
                    v.tensor_copy(nidx[:, b, :], rs_idx[:, b * TB:(b + 1) * TB]).then_inc(L.s_stage, 1)
                with dve.Fori(1, NTB // 2) as i:
                    for b in range(2):
                        dve.wait_ge(L.s_scat[b], i * (16 * TB))
                        v.tensor_copy(nval[:, b, 0:TB * L.H], dnode[:, bass.ds((i * 2 + b) * (TB * L.H), TB * L.H)])
                        v.tensor_copy(nidx[:, b, :], rs_idx[:, bass.ds((i * 2 + b) * TB, TB)]).then_inc(L.s_stage, 1)

            def head(a, L, h, t0=0, t1=T):
                return a.rearrange("p (t h) -> p t h", h=L.H)[:, t0:t1, h]

            def scan(o, keep, add, init, op0=ALU.mult, op1=ALU.add):
                return v.tensor_tensor_scan(o, keep, add, init, op0, op1)

            def edge_loop_attention(L):
                rows, G = rows_of(L), gath(L)
                H, D = L.H, L.D
                mo, ao = H + H * D, 2 * H + H * D
                g3 = lambda a: a.rearrange("p (t h) -> p t h", h=H)
                X0, X1 = ex[:, 0, 0:T * H], ex[:, 1, 0:T * H]
                em = g3(emax[:, 0:(T + 1) * H])
                acc = ph[:, :, 0:H * D]
                NST = 6 + (L is L1)
                NIN = 32 if L is L1 else 16
                with dve.Fori(0, NCH // 2) as i:
                    for b in range(2):
                        base = i * (2 * NST) + b * NST
                        step = [0]

                        def chain(ins):
                            step[0] += 1
                            ins.then_inc(L.s_chain, 1)
                            dve.wait_ge(L.s_chain, base + step[0])

                        c0 = (i * 2 + b) * T
                        v.tensor_copy(nb[:, :], notb[:, bass.ds(c0, T)])
                        chain(v.tensor_scalar(negb[:, :], notb[:, bass.ds(c0, T)], 1.0, BIG, ALU.subtract, ALU.mult))
                        dve.wait_ge(L.s_in[b], (i + 1) * NIN)
                        dve.wait_ge(L.s_g[b], (i + 1) * (16 * T))
                        dve.wait_ge(L.s_st[b], (i + 1) * 16)
                        for h in range(H):
                            scan(head(dsc[:, b, 0:T * H], L, h), nb[:, :], head(dput[:, b, 0:T * H], L, h),
                                 head(dsc[:, 1 - b, 0:T * H], L, h, T - 1, T))
                            last = scan(rows[:, b, :, mo + h], negb[:, :], G[:, b, :, H * 0 + D + h],
                                        rows[:, 1 - b, T - 1:T, mo + h], ALU.add, ALU.max)
                        chain(last)
                        v.tensor_tensor(g3(lgt[:, 0, 0:T * H]), G[:, b, :, D:D + H], g3(dsc[:, b, 0:T * H]), ALU.add)
                        chain(v.tensor_tensor(g3(lgt[:, 1, 0:T * H]), rows[:, b, :, mo:mo + H], g3(dsc[:, b, 0:T * H]), ALU.add))
                        leaky(X0, lgt[:, 0, 0:T * H])
                        chain(leaky(emax[:, H:(T + 1) * H], lgt[:, 1, 0:T * H]))
                        v.tensor_tensor(X0, X0, emax[:, H:(T + 1) * H], ALU.subtract)
                        chain(v.tensor_tensor(X1, emax[:, 0:T * H], emax[:, H:(T + 1) * H], ALU.subtract))
                        v.tensor_tensor(g3(X1), g3(X1), bc(negb[:, :].unsqueeze(2), [P, T, H]), ALU.add).then_inc(L.s_e, 1)
                        v.tensor_copy(emax[:, 0:H], emax[:, T * H:(T + 1) * H])
                        if L is L1:
                            at = attr[:, b, :].rearrange("p (t f) -> p t f", f=FEAT)
                            for f in range(FEAT):
                                scan(rows[:, b, :, ao + f], nb[:, :], at[:, :, f], rows[:, 1 - b, T - 1:T, ao + f])
                            tmp = prod[:, 0:T * FEAT].rearrange("p (t f) -> p t f", f=FEAT)
                            chain(v.tensor_tensor(tmp, at, bc(wv[:, 1, :].unsqueeze(1), [P, T, FEAT]), ALU.mult))
                            v.tensor_reduce(tE[:, bass.ds(c0, T)], tmp, AX_X, ALU.add)
                        dve.wait_ge(L.s_ed, i * 2 + (b + 1))
                        chain(v.tensor_tensor(acc.rearrange("p t (h d) -> p t h d", h=H),
                                              bc(G[:, b, :, 0:D].unsqueeze(2), [P, T, H, D]),
                                              bc(g3(X0).unsqueeze(3), [P, T, H, D]), ALU.mult))
                        for h in range(H):
                            scan(rows[:, b, :, h], head(X1, L, h), head(X0, L, h), rows[:, 1 - b, T - 1:T, h])
                            for j in range(D):
                                f = h * D + j
                                last = scan(rows[:, b, :, H + f], head(X1, L, h), acc[:, :, f], rows[:, 1 - b, T - 1:T, H + f])
                        last.then_inc(L.s_rows, 1)
                        dve.wait_ge(L.s_rows, i * 2 + (b + 3))
                        assert step[0] == NST

            def edge_loop_relation(L):
                rows, G = rows_of(L), gath(L)
                msg = ph[:, :, 0:FEAT]
                NST = 3 + G4
                with dve.Fori(0, NCH // 2) as i:
                    for b in range(2):
                        base = i * (2 * NST) + b * NST
                        step = [0]

                        def chain(ins):
                            step[0] += 1
                            ins.then_inc(L.s_chain, 1)
                            dve.wait_ge(L.s_chain, base + step[0])

                        def onehot(g):
                            dve.wait_ge(s_B, i * (2 * G4) + (g + 1))
                            v.tensor_scalar(oh[:, g % 2, :], ps[:, g % 2, :], ip[:, 0:1], None, ALU.is_equal).then_inc(s_oh, 1)

                        c0 = (i * 2 + b) * T
                        v.tensor_copy(nb[:, :], notb[:, bass.ds(c0, T)])
                        dve.wait_ge(L.s_in[b], (i + 1) * 32)
                        dve.wait_ge(L.s_g[b], (i + 1) * (16 * T))
                        dve.wait_ge(L.s_st[b], (i + 1) * 16)
                        chain(v.tensor_tensor(ef[:, :], G[:, b, :, FEAT], tE[:, bass.ds(c0, T)], ALU.add))
                        chain(scan(dsc[:, b, 0:T], nb[:, :], dput[:, b, 0:T], dsc[:, 1 - b, T - 1:T]))
                        v.tensor_tensor(ef[:, :], ef[:, :], dsc[:, b, 0:T], ALU.add)
                        onehot(b * G4)
                        for g in range(b * G4, (b + 1) * G4):
                            if g + 1 < (b + 1) * G4:
                                onehot(g + 1)
                            t0 = (g % G4) * 4
                            dve.wait_ge(s_Wr, i * (2 * G4) + (g + 1))
                            dve.wait_ge(s_wfree, i * (2 * G4) + (g + 2))
                            w = ps[:, 4 + 2 * (g % 2):6 + 2 * (g % 2), :].rearrange("p b (t i o) -> p (b t) i o", t=2, i=FEAT)
                            pr = prod[:, :].rearrange("p (t i o) -> p t i o", t=4, i=FEAT)
                            chain(v.tensor_tensor(pr, w, bc(G[:, b, t0:t0 + 4, 0:FEAT].unsqueeze(3), [P, 4, FEAT, FEAT]), ALU.mult))
                            v.tensor_reduce(msg[:, t0:t0 + 4, :], pr.rearrange("p t i o -> p t o i"), AX_X, ALU.add)\
                             .then_inc(s_wfree, 1)
                        dve.wait_ge(s_wfree, i * (2 * G4) + ((b + 1) * G4 + 2))
                        chain(v.tensor_tensor(msg, msg, bc(ef[:, :].unsqueeze(2), [P, T, FEAT]), ALU.mult))
                        for f in range(FEAT):
                            last = scan(rows[:, b, :, f], nb[:, :], msg[:, :, f], rows[:, 1 - b, T - 1:T, f])
                        last.then_inc(L.s_rows, 1)
                        dve.wait_ge(L.s_rows, i * 2 + (b + 3))
                        assert step[0] == NST

            def edge_loop_sum(L):
                rows, G = rows_of(L), gath(L)
                with dve.Fori(0, NCH // 2) as i:
                    for b in range(2):
                        v.tensor_copy(nb[:, :], notb[:, bass.ds((i * 2 + b) * T, T)]).then_inc(L.s_chain, 1)
                        dve.wait_ge(L.s_chain, i * 2 + (b + 1))
                        dve.wait_ge(L.s_g[b], (i + 1) * (16 * T))
                        dve.wait_ge(L.s_st[b], (i + 1) * 16)
                        for f in range(FEAT):
                            last = scan(rows[:, b, :, f], nb[:, :], G[:, b, :, f], rows[:, 1 - b, T - 1:T, f])
                        last.then_inc(L.s_rows, 1)
                        dve.wait_ge(L.s_rows, i * 2 + (b + 3))

            def mend_sums(L, c0, c1):
                lr = last_rows(L)[:, :, c0:c1]
                link(v.tensor_tensor(lr, lr, bc(mask[:, :].unsqueeze(2), [P, P, c1 - c0]), ALU.mult))
                link(v.tensor_reduce(crow[:, c0:c1], lr.rearrange("p q f -> p f q"), AX_X, ALU.add))
                dve.wait_ge(L.s_fr, 16)
                link(v.tensor_tensor(frow[:, c0:c1], frow[:, c0:c1], crow[:, c0:c1], ALU.add))

            def mend_attention(L):
                H, D = L.H, L.D
                mo = H + H * D
                lr = last_rows(L)
                F = lambda n, h=None: fx[:, n * H:(n + 1) * H] if h is None else fx[:, n * H + h:n * H + h + 1]
                for h in range(H):
                    link(v.tensor_tensor(sq1[:, :], lr[:, :, mo + h], negmask[:, :], ALU.add))
                    link(v.tensor_reduce(F(2, h), sq1[:, :], AX_X, ALU.max))
                    link(v.tensor_tensor(F(3, h), F(2, h), dfv[:, h:h + 1], ALU.add))
                    link(leaky(F(4, h), F(3, h)))
                    link(v.tensor_scalar(sq1[:, :], lr[:, :, mo + h], dfv[:, h:h + 1], None, ALU.add))
                    link(leaky(sq2[:, :], sq1[:, :]))
                    ask(v.tensor_scalar(sq2[:, :], sq2[:, :], F(4, h), 0.0, ALU.subtract, ALU.min))
                    link(v.tensor_tensor(sq2[:, :], sq2[:, :], mask[:, :], ALU.mult))
                    for c0, c1 in ((h, h + 1), (H + h * D, H + (h + 1) * D)):
                        link(v.tensor_tensor(lr[:, :, c0:c1], lr[:, :, c0:c1], bc(sq2[:, :].unsqueeze(2), [P, P, c1 - c0]), ALU.mult))
                        link(v.tensor_reduce(crow[:, c0:c1], lr[:, :, c0:c1].rearrange("p q f -> p f q"), AX_X, ALU.add))
                dve.wait_ge(L.s_fr, 16)
                fm = frow[:, mo:mo + H]
                link(v.tensor_tensor(F(5), fm, F(2), ALU.max))
                link(v.tensor_tensor(F(3), F(5), dfv[:, 0:H], ALU.add))
                link(leaky(F(6), F(3)))
                link(v.tensor_tensor(F(3), fm, dfv[:, 0:H], ALU.add))
                link(leaky(F(7), F(3)))
                v.tensor_tensor(F(0), F(7), F(6), ALU.subtract)
                ask(v.tensor_tensor(F(1), F(4), F(6), ALU.subtract))
                v.tensor_copy(fm, F(5))
                for r, n in ((frow, 0), (crow, 1)):
                    v.tensor_tensor(r[:, 0:H], r[:, 0:H], F(n), ALU.mult)
                    a = r[:, H:mo].rearrange("p (h d) -> p h d", h=H)
                    last = v.tensor_tensor(a, a, bc(F(n).unsqueeze(2), [P, H, D]), ALU.mult)
                link(last)
                link(v.tensor_tensor(frow[:, 0:mo], frow[:, 0:mo], crow[:, 0:mo], ALU.add))

            def collect(L):
                with dve.Fori(0, NTB // 2) as i:
                    for b in range(2):
                        dve.wait_ge(L.s_ng[b], (i + 1) * (16 * TB))
                        v.tensor_copy(arena[:, bass.ds((i * 2 + b) * (TB * L.W), TB * L.W)], nrow[:, b, 0:TB * L.W])\
                         .then_inc(L.s_nf, 1)
                dve.wait_ge(L.s_nf, NTB + 2)

            def finish_attention(L):
                H, D = L.H, L.D
                mo = H + H * D
                NR = node_rows(L)
                M1, LM = kh(nm[:, 0:K * H], H), kh(nm[:, K * H:2 * K * H], H)
                XN, XS = kh(nex[:, 0:K * H], H), kh(nex[:, K * H:2 * K * H], H)
                s, d = kh(snode, H), kh(dnode, H)
                m = NR[:, :, mo:mo + H]
                link(v.tensor_scalar(nt[:, 0, :], has[:, :], 1.0, BIG, ALU.subtract, ALU.mult))
                link(v.tensor_tensor(m, m, bc(nt[:, 0, :].unsqueeze(2), [P, K, H]), ALU.add))
                link(v.tensor_tensor(M1, m, s, ALU.max))
                link(v.tensor_tensor(M1, M1, d, ALU.add))
                link(leaky(LM, M1))
                v.tensor_tensor(XN, m, d, ALU.add)
                link(v.tensor_tensor(M1, s, d, ALU.add))
                leaky(XN, XN)
                link(leaky(XS, M1))
                v.tensor_tensor(XN, XN, LM, ALU.subtract)
                ask(v.tensor_tensor(XS, XS, LM, ALU.subtract))
                z = NR[:, :, 0:H]
                link(v.tensor_tensor(z, z, XN, ALU.mult))
                link(v.tensor_tensor(z, z, XS, ALU.add))
                link(v.tensor_scalar(LM, z, 1e-16, None, ALU.add))
                link(v.reciprocal(nm[:, 0:K * H], nm[:, K * H:2 * K * H]))
                own = (lambda h: hs3) if L is L1 else (lambda h: tab3(L2.table)[:, :, 0:C2])
                for h in range(H):
                    a = NR[:, :, H + h * D:H + (h + 1) * D]
                    t = scanbuf[:, 0:K * D].rearrange("p (k d) -> p k d", d=D)
                    link(v.tensor_tensor(a, a, bc(XN[:, :, h:h + 1], [P, K, D]), ALU.mult))
                    link(v.tensor_tensor(t, own(h), bc(XS[:, :, h:h + 1], [P, K, D]), ALU.mult))
                    link(v.tensor_tensor(a, a, t, ALU.add))
                    link(v.tensor_tensor(a, a, bc(M1[:, :, h:h + 1], [P, K, D]), ALU.mult))

            def linear(s, src, width, out2):
                with dve.Fori(0, NPAIR) as i:
                    v.tensor_copy(stg[:, 0:2 * width], src[:, bass.ds(i * (2 * width), 2 * width)]).then_inc(s[2], 1)
                    dve.wait_ge(s[0], i * 2 + 2)
                    v.tensor_copy(out2[:, bass.ds(i * (2 * FEAT), 2 * FEAT)], ps[:, 3, 0:2 * FEAT]).then_inc(s[2], 1)
                dve.wait_ge(s[2], 2 * NPAIR)

            link(v.memset(scanbuf[:, :], 0.0))
            dve.sem_inc(L1.s_rows, 2)
            stage_dst(L1)
            edge_loop_attention(L1)
            dve.wait_ge(L1.s_last, 32)
            mend_attention(L1)
            mend_sums(L1, L1.W - FEAT, L1.W)
            dve.sem_inc(L1.s_mend, 1)
            collect(L1)
            finish_attention(L1)
            link(v.tensor_scalar(nt[:, 0, :], cnt[:, :], 1.0, None, ALU.max))
            link(v.reciprocal(nt[:, 1, :], nt[:, 0, :]))
            link(v.tensor_tensor(nt[:, 1, :], nt[:, 1, :], has[:, :], ALU.mult))
            am = node_rows(L1)[:, :, L1.W - FEAT:]
            link(v.tensor_tensor(am, am, bc(nt[:, 1, :].unsqueeze(2), [P, K, FEAT]), ALU.mult))
            link(v.tensor_tensor(xs3, xs3, am, ALU.add))
            mlp_chain = sem("mlp_chain")
            with dve.Fori(0, NPAIR) as i:
                v.tensor_copy(stg[:, :].rearrange("p (k c) -> p k c", k=2),
                              arena[:, bass.ds(i * (2 * L1.W), 2 * L1.W)].rearrange("p (k c) -> p k c", k=2)[:, :, H1:H1 + AH])\
                 .then_inc(s_ms, 1)
                dve.wait_ge(s_ma, i + 1)
                v.tensor_scalar(hT[0:HC1, 0, :], hT[0:HC1, 0, :], 1.0, 1.0, ALU.min, ALU.subtract).then_inc(mlp_chain, 1)
                dve.wait_ge(mlp_chain, i + 1)
                v.scalar_tensor_tensor(out=hT[0:HC1, 0, :], in0=hT[0:HC1, 0, :], scalar=LAMALPHA, in1=hT[0:HC1, 1, :],
                                       op0=ALU.mult, op1=ALU.add).then_inc(s_ms, 1)
                dve.wait_ge(s_mpe, i * 3 + 3)
                o = ps[:, 3, 0:2 * (C2 + 2)].rearrange("p (j c) -> p j c", j=2)
                v.tensor_copy(tab[:, bass.ds(i * (2 * (C2 + 1)), 2 * (C2 + 1))].rearrange("p (j c) -> p j c", j=2), o[:, :, 0:C2 + 1])
                v.tensor_copy(dnode[:, bass.ds(i * 2, 2)], o[:, :, C2 + 1]).then_inc(mlp_out, 1)
            dve.wait_ge(mlp_out, NPAIR)

            link(v.tensor_copy(kh(snode, 1), tab3(L2.table)[:, :, C2:C2 + 1]))
            link(v.memset(scanbuf[:, :], 0.0))
            dve.sem_inc(L2.s_rows, 2)
            v.memset(dsc[:, :, :], 0.0)
            link(v.memset(emax[:, :], 0.0))
            dve.sem_inc(L2.s_tab, 1)
            stage_dst(L2)
            edge_loop_attention(L2)
            dve.wait_ge(L2.s_last, 32)
            mend_attention(L2)
            dve.sem_inc(L2.s_mend, 1)
            collect(L2)
            finish_attention(L2)
            u = node_rows(L2)[:, :, 1:1 + C2]
            o2 = scanbuf[:, 0:K * C2].rearrange("p (k c) -> p k c", c=C2)
            r2 = scanbuf[:, K * C2:2 * K * C2].rearrange("p (k c) -> p k c", c=C2)
            link(v.tensor_tensor(u, u, bc(b2b[:, :].unsqueeze(1), [P, K, C2]), ALU.add))
            v.tensor_scalar(r2, u, LAM, 0.0, ALU.mult, ALU.max)
            ask(v.tensor_copy(o2, u))
            link(v.tensor_scalar(o2, o2, 1.0, 1.0, ALU.min, ALU.subtract))
            link(v.scalar_tensor_tensor(out=scanbuf[:, 0:K * C2], in0=scanbuf[:, 0:K * C2], scalar=LAMALPHA,
                                        in1=scanbuf[:, K * C2:2 * K * C2], op0=ALU.mult, op1=ALU.add))
            linear(lin["head"], scanbuf, C2, hs)
            link(v.tensor_tensor(xs3, xs3, hs3, ALU.add))
            link(v.tensor_tensor(xs3, xs3, bc(bfb[:, :].unsqueeze(1), [P, K, FEAT]), ALU.add))

            layernorm_relu()
            project(kh(snode, 1), wv[:, 0, :], 1)
            project(kh(dnode, 1), wv[:, 2, :], 1)
            v.tensor_copy(tab3(L3.table)[:, :, 0:FEAT], hs3)
            v.tensor_copy(tab3(L3.table)[:, :, FEAT:], kh(snode, 1)).then_inc(L3.s_tab, 1)
            dve.wait_ge(s_wrl, 32)
            link(v.tensor_copy(wsp[:, 0, :], wr[:, 0, :]))
            for part in (1, 2):
                link(v.tensor_tensor(wr[:, 0, :], wr[:, 0, :], wsp[:, part - 1, :], ALU.subtract))
                link(v.tensor_copy(wsp[:, part, :], wr[:, 0, :]))
            link(v.memset(scanbuf[:, :], 0.0))
            dve.sem_inc(L3.s_rows, 2)
            v.memset(dsc[:, :, :], 0.0)
            link(v.tensor_scalar(sel[0:T, :].rearrange("k (t r) -> k t r", t=T),
                                 bc(iq[0:T, 0:T].unsqueeze(2), [T, T, P]), ip[0:T, 0:1], None, ALU.is_equal))
            dve.sem_inc(s_ready, 1)
            stage_dst(L3)
            edge_loop_relation(L3)
            dve.wait_ge(L3.s_last, 32)
            mend_sums(L3, 0, FEAT)
            dve.sem_inc(L3.s_mend, 1)
            collect(L3)

            def add_sums(L, scale):
                a = node_rows(L)
                link(v.tensor_tensor(a, a, bc(scale.unsqueeze(2), [P, K, FEAT]), ALU.mult))
                link(v.tensor_tensor(xs3, xs3, a, ALU.add))

            add_sums(L3, has[:, :])

            layernorm_relu()
            ask(v.tensor_scalar(nt[:, 0, :], cnt[:, :], 1.0, None, ALU.add))
            link(v.reciprocal(nt[:, 1, :], nt[:, 0, :]))
            linear(lin["gcnw"], hs, FEAT, tab)
            link(v.memset(scanbuf[:, :], 0.0))
            dve.sem_inc(L4.s_rows, 2)
            v.tensor_tensor(tab3(FEAT), tab3(FEAT), bc(nt[:, 1, :].unsqueeze(2), [P, K, FEAT]), ALU.mult).then_inc(L4.s_tab, 1)
            edge_loop_sum(L4)
            dve.wait_ge(L4.s_last, 32)
            mend_sums(L4, 0, FEAT)
            dve.sem_inc(L4.s_mend, 1)
            collect(L4)
            a4 = node_rows(L4)
            link(v.tensor_tensor(a4, a4, bc(has[:, :].unsqueeze(2), [P, K, FEAT]), ALU.mult))
            link(v.tensor_tensor(a4, a4, tab3(FEAT), ALU.add))
            link(v.tensor_tensor(xs3, xs3, bc(b3b[:, :].unsqueeze(1), [P, K, FEAT]), ALU.add))
            add_sums(L4, nt[:, 1, :])
            dve.sem_inc(s_fin, 1)


_INS = ["x", "src", "dst", "edge_attr_16", "edge_type_90", "L0_gnn_W1", "L0_gnn_a_src1", "L0_gnn_a_dst1", "L0_gnn_b1",
        "L0_gnn_W2", "L0_gnn_a_src2", "L0_gnn_a_dst2", "L0_gnn_b2", "L0_gnn_Wf", "L0_gnn_bf", "L2_gnn_Ws", "L2_gnn_Wa",
        "L2_gnn_weight", "L2_gnn_w_comp", "L3_gnn_W", "L3_gnn_b"]


def kernel(**inputs):
    import numpy as _np
    import concourse.bacc as _bacc
    from concourse import mybir as _mybir
    from concourse.bass_utils import run_bass_kernel_spmd as _run

    nc = _bacc.Bacc("TRN2", target_bir_lowering=False, num_devices=1)
    arrays, args = {}, []
    for name in _INS:
        a = _np.ascontiguousarray(inputs[name])
        arrays[f"in_{name}_dram"] = a
        args.append(nc.dram_tensor(f"in_{name}_dram", a.shape, _mybir.dt.from_np(a.dtype), kind="ExternalInput").ap())
    shape = inputs["x"].shape
    args.append(nc.dram_tensor("out_0_dram", shape, _mybir.dt.from_np(_np.dtype("float32")), kind="ExternalOutput").ap())
    gnn_kernel(nc, *args)
    r = _run(nc, [arrays], core_ids=[0])
    return r.results[0]["out_0_dram"]
```

```python
from contextlib import ExitStack

import concourse.bass as bass
from concourse import mybir

ALU = mybir.AluOpType
ACT = mybir.ActivationFunctionType
AX_X = mybir.AxisListType.X
F32 = mybir.dt.float32
BF16 = mybir.dt.bfloat16
I32 = mybir.dt.int32
RMAX = bass.bass_isa.ReduceOp.max

P = 128
T = 52
TB = 7
TP = 2 * TB
TH = 26
AHEAD = 18
FEAT = 16
SLOPE = 0.2
BIG = 1.0e30
SKIP = float(1 << 23)
RNE = 12582912.0
LAM = 1.0507009873554805
LAMALPHA = LAM * 1.6732632423543772


class Layer:

    def __init__(self, name, heads, feat, table, width, has_dst):
        self.name, self.H, self.D, self.table, self.W, self.has_dst = name, heads, feat, table, width, has_dst


def gnn_kernel(nc, x, src, dst, edge_attr, edge_type, W1, a_src1, a_dst1, b1, W2, a_src2, a_dst2, b2,
               Wf, bf, Ws, Wa, weight, w_comp, W3, b3, out):
    N, _ = x.shape
    E, = src.shape
    K = -(-N // P)
    NP = P * K
    C = -(-E // (P * 2 * T)) * 2 * T
    EP = P * C
    NCH = C // T
    NTB = K // TB
    H1, C1 = a_src1.shape
    C2 = a_src2.shape[1]
    HC1 = H1 * C1
    R, B = w_comp.shape
    G4 = T // 4
    M2 = FEAT * FEAT
    ELAST = E - (P - 1) * C
    NLAST = N - (P - 1) * K
    assert K % (2 * TB) == 0 and NCH % 2 == 0 and T % 4 == 0 and C % (2 * TH) == 0 and 0 < ELAST <= C
    assert AHEAD % 2 == 0 and AHEAD < NCH
    WLOADS = 25 + H1
    AH = H1 * FEAT
    L1 = Layer("gat1", H1, FEAT, FEAT + H1, 2 * H1 + AH + FEAT, True)
    L2 = Layer("gat2", 1, C2, C2 + 1, 2 + C2, True)
    L3 = Layer("rel", 1, FEAT, FEAT + 1, 2 * FEAT, False)
    L4 = Layer("gcn", 1, FEAT, FEAT, FEAT, False)
    LAYERS = [L1, L2, L3, L4]
    WMAX = L1.W

    with ExitStack() as ctx:
        def sb(name, shape, dt=F32):
            return ctx.enter_context(nc.sbuf_tensor(name, shape, dt))

        def sem(name):
            return ctx.enter_context(nc.semaphore(name))

        def dram(name, shape, dt=F32):
            return nc.dram_tensor(name, shape, dt, kind="Internal").ap()

        e_src, e_dst, e_typ = (dram(f"e_{n}", [EP, 1], I32) for n in ("src", "dst", "typ"))
        e_attr = dram("e_attr", [EP, FEAT])
        next_slot = dram("next_slot", [NP, 1])
        rowend_d = dram("rowend_d", [NP, 1])
        dlast_d = dram("dlast_d", [P, 1])
        wrel_d = dram("wrel_d", [FEAT * R, FEAT])
        spill = dram("spill", [EP, L1.table])
        for L in LAYERS:
            L.tab = dram(f"tab_{L.name}", [NP, L.table])
            L.scan = dram(f"scan_{L.name}", [EP, L.W])
            L.last_d = dram(f"last_{L.name}", [P, L.W])
            if L.has_dst:
                L.dnode = dram(f"dnode_{L.name}", [NP, L.H])
                L.dput = dram(f"dput_{L.name}", [EP, L.H])

        notb = sb("notb", [P, C])
        dst_f = sb("dst_f", [P, C])
        tE = sb("tE", [P, C])
        dst_i = tE[:, :].bitcast(I32)
        arena = sb("arena", [P, P * WMAX])
        scanbuf = sb("scanbuf", [P, 2 * T * WMAX])
        gbuf = sb("gbuf", [P, 2 * T * L2.table])
        gin = dst_f[:, 0:2 * T * L1.table].rearrange("p (b f) -> p b f", b=2)
        idx = sb("idx", [P, 2, T], I32)
        dput = sb("dput", [P, 2, T * H1])
        attr = sb("attr", [P, 2, T * FEAT])
        typ = sb("typ", [P, 2, T], I32)
        ph = sb("ph", [P, T, AH])
        dsc = sb("dsc", [P, 2, T * H1])
        lgt = sb("lgt", [P, 2, T * H1])
        ex = sb("ex", [P, 2, T * H1])
        emax = sb("emax", [P, (T + 1) * H1])
        nb = sb("nb", [P, T])
        negb = sb("negb", [P, T])
        iq_i = sb("iq_i", [P, P], I32)
        ip_i = sb("ip_i", [P, 1], I32)
        iq = sb("iq", [P, P])
        ip = sb("ip", [P, 1])
        iqb = sb("iqb", [P, P], BF16)
        ident = sb("ident", [P, P])
        lower = sb("lower", [P, P])
        mask = sb("mask", [P, P])
        negmask = sb("negmask", [P, P])
        sq1 = sb("sq1", [P, P])
        sq2 = sb("sq2", [P, P])
        hd = sb("hd", [P, 4, TH])
        cnt = sb("cnt", [P, K])
        has = sb("has", [P, K])
        re = sb("re", [P, K])
        rs = sb("rs", [P, K])
        nt = sb("nt", [P, 2, K])
        rs_idx = sb("rs_idx", [P, K], I32)
        re_idx = sb("re_idx", [P, K], I32)
        nidx = sb("nidx", [P, 2, TB], I32)
        nval = sb("nval", [P, 2, TB * H1])
        selu_e = scanbuf[:, (K + TP) * C2:(K + 2 * TP) * C2]
        selu_r = scanbuf[:, (K + 2 * TP) * C2:(K + 3 * TP) * C2]
        nrow = sb("nrow", [P, 2, TB * WMAX])
        flag = sb("flag", [P, 4])
        flag_i = sb("flag_i", [P, 1], I32)
        nxt = sb("nxt", [P, 1], I32)
        dfirst_i = sb("dfirst_i", [P, 1], I32)
        fix_i = sb("fix_i", [P, 1], I32)
        col = sb("col", [P, 16])
        xs = sb("xs", [P, K * FEAT])
        hs = sb("hs", [P, K * FEAT])
        tab = sb("tab", [P, K * (C2 + 2)])
        snode = sb("snode", [P, K * H1])
        dnode = sb("dnode", [P, K * H1])
        nex = sb("nex", [P, 2 * TP * H1])
        nm = sb("nm", [P, 2 * TP * H1])
        dfv = sb("dfv", [P, H1])
        frow = sb("frow", [P, WMAX])
        crow = sb("crow", [P, WMAX])
        fx = sb("fx", [P, 8 * H1])
        W1b = scanbuf[:, 0:FEAT * HC1]
        as1 = sb("as1", [P, 2, HC1])
        ws1 = sb("ws1", [P, 2, AH])
        W1bd = sb("W1bd", [AH, HC1])
        b1c = sb("b1c", [HC1, 2])
        W2e = sb("W2e", [HC1, C2 + 2])
        as2 = sb("as2", [HC1, 2, C2])
        t2 = sb("t2", [HC1, 2, C2])
        b2b = sb("b2b", [P, C2])
        Wf_bd = sb("Wf_bd", [4 * C2, 4 * FEAT])
        bfb = sb("bfb", [P, FEAT])
        Wsb = sb("Wsb", [P, M2])
        Wab = sb("Wab", [P, 3 * FEAT])
        wv = sb("wv", [P, 3, FEAT])
        wvt = sb("wvt", [P, M2])
        wct = sb("wct", [B, R])
        Vs = sb("Vs", [B, FEAT * FEAT])
        wm = sb("wm", [P, M2])
        wr = sb("wr", [P, 2, M2])
        wsp = sb("wsp", [P, 3, M2], BF16)
        W3_bd = sb("W3_bd", [TB * FEAT, TB * FEAT])
        b3b = sb("b3b", [P, FEAT])
        stg = [sb(f"stg{b}", [P, TB * AH])[:, :] for b in range(2)]
        aT = [gbuf[:, 0:TB * P], scanbuf[:, 2 * T * WMAX - TB * P:]]
        hT = [a.rearrange("p (q c) -> p q c", q=2) for a in (gbuf[:, TB * P:3 * TB * P], scanbuf[:, K * C2:K * C2 + 2 * TB * P])]
        assert 2 * K * C2 + TB * P <= 2 * T * WMAX
        typ_f = sb("typ_f", [P, T])
        typT = sb("typT", [T, P], BF16)
        oh = sb("oh", [P, 2, 4 * P], BF16)
        prod = sb("prod", [P, 4 * M2])
        ef = sb("ef", [P, T])
        sel = scanbuf[:, 2 * T * L2.W:2 * T * L2.W + T * P // 2].bitcast(BF16)
        oneA = scanbuf[:, 0:TH * P].bitcast(BF16)
        oneB = scanbuf[:, TH * P:TH * P + TH * K].bitcast(BF16)

        ps = ctx.enter_context(nc.psum_tensor("ps", [P, 8, 512], F32))
        ps_turn = [ps[:, c:c + 2, :].rearrange("p b c -> p (b c)")[:, 0:TB * P] for c in (1, 4)]
        ps_out = [ps[:, 3, :], ps[:, 6, :]]

        s_arena = sem("arena_zeros")
        s_iota, s_pad, s_v = sem("s_iota"), sem("s_pad"), sem("s_v")
        s_dst_in, s_x, s_w = sem("s_dst_in"), sem("s_x"), sem("s_w")
        s_zero, s_zfill, s_viol, s_allred, s_tail = (sem(n) for n in ("s_zero", "s_zfill", "s_viol", "s_allred", "s_tail"))
        s_onehot, s_hist = sem("s_onehot"), sem("s_hist")
        s_rows, s_rowsst, s_copy, s_copyattr, s_edges, s_dstre = (sem(n) for n in ("s_rows", "s_rowsst", "s_copy", "s_copyattr", "s_edges", "s_dstre"))
        s_spill = [sem(f"spill{b}") for b in range(2)]
        s_dends, s_dlb, s_ref = (sem(n) for n in ("s_dends", "s_dlb", "s_ref"))
        s_wm, s_wmc, s_wrl = (sem(n) for n in ("s_wm", "s_wmc", "s_wrl"))
        s_fin, s_out = sem("s_fin"), sem("s_out")
        s_exq, s_exd = sem("s_exq"), sem("s_exd")
        for L in LAYERS:
            n = L.name
            L.s_tab, L.s_tabst, L.s_chain, L.s_rows = (sem(f"{q}_{n}") for q in ("tab", "tabst", "chain", "rows"))
            L.s_idx = [sem(f"idx{b}_{n}") for b in range(2)]
            L.s_g = [sem(f"g{b}_{n}") for b in range(2)]
            L.s_st = [sem(f"st{b}_{n}") for b in range(2)]
            L.s_last, L.s_fr, L.s_mend = (sem(f"{q}_{n}") for q in ("last", "fr", "mend"))
            L.s_ni, L.s_nf = sem(f"ni_{n}"), sem(f"nf_{n}")
            L.s_ng = [sem(f"ng{b}_{n}") for b in range(2)]
            if L.has_dst:
                L.s_stage, L.s_df, L.s_dput = sem(f"stage_{n}"), sem(f"df_{n}"), sem(f"dput_{n}")
                L.s_scat = [sem(f"scat{b}_{n}") for b in range(2)]
            if L is not L4:
                L.s_in = [sem(f"in{b}_{n}") for b in range(2)]
            if L is L1 or L is L2:
                L.s_e, L.s_ed = sem(f"e_{n}"), sem(f"ed_{n}")
        s_lt, mlp_out, mlp_chain = sem("sort_lt"), sem("mlp_out"), sem("mlp_chain")
        s_mpe, s_mc, s_ma, s_ms = (sem(n) for n in ("mlp_pe", "mlp_c", "mlp_a", "mlp_s"))
        lin = {n: [sem(f"{n}_{q}") for q in ("pe", "c", "f")] for n in ("head", "gcnw")}
        s_ready = sem("ready")
        s_past, s_pe_past = sem("pool_past"), sem("pe_past")
        s_tyf, s_tyt, s_tyc, s_B, s_oh, s_Wr, s_wfree = (sem(n) for n in ("tyf", "tyt", "tyc", "rel_B", "rel_oh", "rel_W", "rel_free"))

        def edges(a):
            return a.rearrange("(p c) f -> p (c f)", p=P)

        def nodes(a):
            return a.rearrange("(p k) f -> p (k f)", p=P)

        xs3 = xs[:, :].rearrange("p (k i) -> p k i", i=FEAT)
        hs3 = hs[:, :].rearrange("p (k i) -> p k i", i=FEAT)

        def rows_of(L):
            return scanbuf[:, 0:2 * T * L.W].rearrange("p (b t f) -> p b t f", b=2, t=T)

        def gath(L):
            return gbuf[:, 0:2 * T * L.table].rearrange("p (b t f) -> p b t f", b=2, t=T)

        def last_rows(L):
            return arena[:, 0:P * L.W].rearrange("p (q f) -> p q f", q=P)

        def node_rows(L):
            return arena[:, 0:K * L.W].rearrange("p (k f) -> p k f", k=K)

        def tab3(w):
            return tab[:, 0:K * w].rearrange("p (k f) -> p k f", k=K)

        def kh(a, h):
            return a[:, 0:K * h].rearrange("p (k h) -> p k h", h=h)

        def groups(width):
            n = min(P // width, TB)
            return [(c, min(n, TB - c)) for c in range(0, TB, n)]

        def bc(a, shape):
            return a.to_broadcast(shape)

        sort_sems = [sem(f"sort{n}") for n in range(12)]
        so_i = sb("so_i", [P, 4], I32)
        so_row = sb("so_row", [P, P], I32)
        so_attr = sb("so_attr", [P, FEAT])
        so_f = sb("so_f", [P, 8])
        so_eq = sb("so_eq", [P, 2, P])
        so_lt = sb("so_lt", [P, P])
        so_pos = sb("so_pos", [P, 2], I32)

        def sort_edges(pool):
            s_ld = sort_sems[0:5]
            s_cnt, s_op, s_cn = sort_sems[5:8]
            s_sc = sort_sems[8:12]
            g = nc.gpsimd
            pool.wait_ge(s_rowsst, 32)
            full = E // P
            OPS = 14

            def tile(i, n):
                e0 = i * P
                part = lambda a: a[bass.ds(e0, n)].rearrange("(p o) -> p o", o=1)
                pool.dma_start(so_i[0:n, 0:1], part(dst)).then_inc(s_ld[0], 16)
                pool.dma_start(so_i[0:n, 1:2], part(src)).then_inc(s_ld[1], 16)
                pool.dma_start(so_i[0:n, 2:3], part(edge_type)).then_inc(s_ld[2], 16)
                pool.dma_start(so_attr[0:n, :], edge_attr[bass.ds(e0, n), :]).then_inc(s_ld[3], 16)
                pool.dma_start(so_row[0:n, 0:n], dst[bass.ds(e0, n)].partition_broadcast(n)).then_inc(s_ld[4], 16)
                for s in s_ld:
                    pool.wait_ge(s, (i + 1) * 16)
                pool.sem_inc(s_past, 1)
                pool.indirect_dma_start(out=so_f[0:n, 0:1], out_offset=None, in_=next_slot,
                                        in_offset=bass.IndirectOffsetOnAxis(ap=so_i[0:n, 0:1], axis=0)).then_inc(s_cnt, 16)
                ops = [0]

                def chain(ins):
                    ops[0] += 1
                    ins.then_inc(s_op, 1)
                    pool.wait_ge(s_op, i * OPS + ops[0])

                f = lambda c: so_f[0:n, c:c + 1]
                g.tensor_copy(f(1), so_i[0:n, 0:1])
                chain(g.tensor_copy(so_eq[0:n, 0, 0:n], so_row[0:n, 0:n]))
                pool.sem_inc(s_past, 1)
                chain(g.tensor_scalar(so_eq[0:n, 1, 0:n], so_eq[0:n, 0, 0:n], f(1), None, ALU.is_equal))
                chain(g.tensor_tensor(so_eq[0:n, 0, 0:n], so_eq[0:n, 1, 0:n], so_lt[0:n, 0:n], ALU.mult))
                w = P
                while w > 1:
                    w //= 2
                    chain(g.tensor_tensor(so_eq[0:n, :, 0:w], so_eq[0:n, :, 0:w], so_eq[0:n, :, w:2 * w], ALU.add))
                pool.wait_ge(s_cnt, (i + 1) * 16)
                g.tensor_tensor(f(2), f(0), so_eq[0:n, 0, 0:1], ALU.add)
                g.tensor_tensor(f(3), f(0), so_eq[0:n, 1, 0:1], ALU.add)
                chain(g.tensor_tensor(f(4), so_eq[0:n, 1, 0:1], so_eq[0:n, 0, 0:1], ALU.subtract))
                pool.sem_inc(s_past, 1)
                g.tensor_copy(so_pos[0:n, 0:1], f(2))
                chain(g.tensor_scalar(f(5), f(4), SKIP, -SKIP, ALU.mult, ALU.add))
                chain(g.tensor_tensor(f(6), f(5), f(1), ALU.add))
                pool.sem_inc(s_past, 1)
                chain(g.tensor_copy(so_pos[0:n, 1:2], f(6)))
                assert ops[0] == OPS
                pool.sem_inc(s_past, 1)
                pool.indirect_dma_start(out=next_slot, out_offset=bass.IndirectOffsetOnAxis(ap=so_pos[0:n, 1:2], axis=0),
                                        in_=f(3), in_offset=None, bounds_check=NP - 1, oob_is_err=False).then_inc(s_cn, 16)
                for q, (o, a) in enumerate(((e_dst, so_i[0:n, 0:1]), (e_src, so_i[0:n, 1:2]), (e_typ, so_i[0:n, 2:3]),
                                            (e_attr, so_attr[0:n, :]))):
                    pool.indirect_dma_start(out=o, out_offset=bass.IndirectOffsetOnAxis(ap=so_pos[0:n, 0:1], axis=0),
                                            in_=a, in_offset=None).then_inc(s_sc[q], 16)
                for s in (s_cn, *s_sc):
                    pool.wait_ge(s, (i + 1) * 16)
                pool.sem_inc(s_past, 1)

            g.memset(so_lt[:, :], 1.0).then_inc(s_lt, 1)
            pool.wait_ge(s_lt, 1)
            g.affine_select(out=so_lt[:, :], in_=so_lt[:, :], compare_op=ALU.is_gt, fill=0.0, base=0,
                            pattern=[[-1, P]], channel_multiplier=1).then_inc(s_lt, 1)
            pool.wait_ge(s_lt, 2)
            g.memset(so_eq[:, :, :], 0.0).then_inc(s_lt, 1)
            pool.wait_ge(s_lt, 3)
            with pool.Fori(0, full) as i:
                tile(i, P)
            if E % P:
                g.memset(so_eq[:, :, :], 0.0).then_inc(s_lt, 1)
                pool.wait_ge(s_lt, 4)
                tile(full, E % P)

        block = ctx.enter_context(nc.Block())

        @block.sync
        def _(sp):
            sp.wait_ge(s_pad, 1)
            sp.dma_start(dst_i[0:P - 1, :], dst[0:(P - 1) * C].rearrange("(p c) -> p c", c=C)).then_inc(s_dst_in, 16)
            sp.dma_start(dst_i[P - 1:P, 0:ELAST], dst[(P - 1) * C:E].rearrange("(o c) -> o c", o=1)).then_inc(s_dst_in, 16)
            sp.dma_start(nxt[0:P - 1, :], dst[C:(P - 1) * C + 1:C].rearrange("(p o) -> p o", o=1),
                         allow_slow_non_contiguous=True).then_inc(s_dst_in, 16)
            sp.dma_start(xs[0:P - 1, :], x[0:(P - 1) * K, :].rearrange("(p k) i -> p (k i)", k=K)).then_inc(s_x, 16)
            sp.dma_start(xs[P - 1:P, 0:NLAST * FEAT], x[(P - 1) * K:N, :].rearrange("(o k) i -> o (k i)", o=1)).then_inc(s_x, 16)
            for o, i in (
                (as1[:, 0, :], a_src1.rearrange("h c -> (h c)").partition_broadcast(P)),
                (as1[:, 1, :], a_dst1.rearrange("h c -> (h c)").partition_broadcast(P)),
                (b1c[:, 0:1], b1.rearrange("(c o) -> c o", o=1)),
                (W2e[:, 0:C2], W2),
                (as2[:, 0, :], a_src2.rearrange("h c -> (h c)").partition_broadcast(HC1)),
                (as2[:, 1, :], a_dst2.rearrange("h c -> (h c)").partition_broadcast(HC1)),
                (b2b[:, :], b2.partition_broadcast(P)),
                *((Wf_bd[j * C2:(j + 1) * C2, j * FEAT:(j + 1) * FEAT], Wf) for j in range(4)),
                (bfb[:, :], bf.partition_broadcast(P)),
                (Wsb[:, :], Ws.rearrange("o i -> (o i)").partition_broadcast(P)),
                (Wab[:, :], Wa.rearrange("o i -> (o i)").partition_broadcast(P)),
                (Vs[:, :].rearrange("b (a o) -> b a o", a=FEAT),
                 weight.rearrange("b i o -> (b i o)").rearrange("(a b o) -> b a o", a=FEAT, b=B)),
                *((W3_bd[j * FEAT:(j + 1) * FEAT, j * FEAT:(j + 1) * FEAT], W3) for j in range(TB)),
                (b3b[:, :], b3.partition_broadcast(P)),
            ):
                sp.dma_start(o, i).then_inc(s_w, 16)
            sp.dma_start(wct[:, :], w_comp.rearrange("r b -> b r"), allow_slow_non_contiguous=True).then_inc(s_w, 16)
            for h in range(H1):
                sp.dma_start(W1bd[h * FEAT:(h + 1) * FEAT, h * C1:(h + 1) * C1],
                             W1[:, h * C1:(h + 1) * C1]).then_inc(s_w, 16)
            sp.dma_start(W1b, W1.rearrange("i c -> (i c)").partition_broadcast(P)).then_inc(s_w, 16)
            sp.wait_ge(s_arena, 1)
            sp.wait_ge(s_dst_in, 48)
            zrow = arena[0:1, 0:(EP - E) * FEAT]
            sp.dma_start(e_src[E:EP, :].rearrange("e o -> o e"), zrow[:, 0:EP - E].bitcast(I32)).then_inc(s_tail, 16)
            sp.dma_start(e_typ[E:EP, :].rearrange("e o -> o e"), zrow[:, 0:EP - E].bitcast(I32)).then_inc(s_tail, 16)
            sp.dma_start(e_attr[E:EP, :].rearrange("(o e) f -> o (e f)", o=1), zrow).then_inc(s_tail, 16)
            sp.dma_start(e_dst[E:EP, :].rearrange("e o -> o e"), dst_i[P - 1:P, ELAST:C]).then_inc(s_tail, 16)
            for L in LAYERS:
                if L.has_dst:
                    for h in range(L.H):
                        sp.dma_start(edges(L.dput)[:, h * C:(h + 1) * C], arena[:, 0:C]).then_inc(s_zfill, 16)
            sp.wait_ge(s_edges, 1)

            def indices(b, c0):
                sp.dma_start(idx[:, b, :], edges(e_src)[:, bass.ds(c0, T)]).then_inc(L1.s_idx[b], 16)

            def layer(L):
                if L is L1:
                    for b in range(2):
                        indices(b, b * T)
                sp.wait_ge(L.s_tab, 1)
                sp.dma_start(nodes(L.tab), tab[:, 0:K * L.table]).then_inc(L.s_tabst, 16)
                if L is L1:
                    sp.wait_ge(L.s_tab, 2)
                    sp.wait_ge(L.s_tabst, 16)
                if L.has_dst:
                    sp.dma_start(nodes(L.dnode), dnode[:, 0:K * L.H]).then_inc(L.s_tabst, 16)
                if L is L1:
                    gather_ahead()
                else:
                    chunk_inputs(L)
                sp.wait_ge(L.s_rows, NCH + 2)
                sp.dma_start(L.last_d, rows_of(L)[:, 1, T - 1, :]).then_inc(L.s_last, 16)
                sp.wait_ge(L.s_last, 16)
                sp.dma_start(arena[:, 0:P * L.W], L.last_d.rearrange("q f -> (q f)").partition_broadcast(P)).then_inc(L.s_last, 16)

            def gather_ahead():
                def rows_out(b, i, more):
                    sp.wait_ge(L1.s_g[b], (i + 1) * (16 * T))
                    sp.dma_start(edges(spill)[:, bass.ds((i * 2 + b) * (T * L1.table), T * L1.table)],
                                 gbuf[:, b * T * L1.table:(b + 1) * T * L1.table]).then_inc(s_spill[b], 16)
                    if more:
                        sp.wait_ge(s_spill[b], (i + 1) * 16)
                        indices(b, (i * 2 + (b + 2)) * T)

                with sp.Fori(0, NCH // 2 - 1) as i:
                    for b in range(2):
                        rows_out(b, i, True)
                for b in range(2):
                    rows_out(b, NCH // 2 - 1, False)

            def chunk_inputs(L):
                if L.has_dst:
                    sp.wait_ge(L.s_df, 16)
                    for b in range(2):
                        sp.wait_ge(L.s_scat[b], 16 * TB * (NTB // 2))
                    sp.dma_start(edges(L.dput)[:, 0:L.H], dfv[:, 0:L.H], allow_slow_non_contiguous=True).then_inc(L.s_dput, 16)
                    sp.wait_ge(L.s_dput, 16)
                with sp.Fori(0, NCH // 2) as i:
                    for b in range(2):
                        sp.wait_ge(L.s_rows, i * 2 + (b + 1))
                        sp.dma_start(idx[:, b, :], edges(e_src)[:, bass.ds((i * 2 + b) * T, T)]).then_inc(L.s_idx[b], 16)
                        if L.has_dst:
                            sp.dma_start(dput[:, b, 0:T * L.H], edges(L.dput)[:, bass.ds((i * 2 + b) * (T * L.H), T * L.H)])\
                              .then_inc(L.s_in[b], 16)
                        if L is L3:
                            sp.dma_start(typ[:, b, :], edges(e_typ)[:, bass.ds((i * 2 + b) * T, T)]).then_inc(L.s_in[b], 16)

            for L in LAYERS:
                layer(L)
            sp.wait_ge(s_fin, 1)
            sp.dma_start(out[0:(P - 1) * K, :].rearrange("(p k) i -> p (k i)", k=K), xs[0:P - 1, :]).then_inc(s_out, 16)
            sp.dma_start(out[(P - 1) * K:N, :].rearrange("(o k) i -> o (k i)", o=1), xs[P - 1:P, 0:NLAST * FEAT]).then_inc(s_out, 16)
            sp.wait_ge(s_out, 32)

        @block.gpsimd
        def _(pool):
            nc.gpsimd.iota(iq_i[:, :], [[1, P]], base=0, channel_multiplier=0).then_inc(s_iota, 1)
            nc.gpsimd.iota(ip_i[:, :], [[0, 1]], base=0, channel_multiplier=1).then_inc(s_iota, 1)
            nc.gpsimd.memset(arena[:, :], 0.0).then_inc(s_arena, 1)
            pool.wait_ge(s_viol, 1)
            nc.gpsimd.partition_all_reduce(flag[:, 1:2], flag[:, 0:1], P, RMAX).then_inc(s_allred, 1)
            pool.wait_ge(s_allred, 1)
            nc.gpsimd.tensor_copy(flag_i[:, :], flag[:, 1:2]).then_inc(s_allred, 1)
            pool.wait_ge(s_allred, 2)
            unsorted = pool.value_load(flag_i[0:1, 0:1], min_val=0, max_val=1)
            with pool.If(unsorted):
                sort_edges(pool)
            with pool.Else():
                whole = (P - 1) * C
                for o, a in ((e_src, src), (e_dst, dst), (e_typ, edge_type)):
                    pool.dma_start(o[0:whole, :].rearrange("(p c) o -> p (c o)", c=C),
                                   a[0:whole].rearrange("(p c) -> p c", c=C)).then_inc(s_copy, 16)
                    pool.dma_start(o[whole:E, :].rearrange("e o -> o e"),
                                   a[whole:E].rearrange("(o e) -> o e", o=1)).then_inc(s_copy, 16)
                pool.dma_start(e_attr[0:E, :], edge_attr).then_inc(s_copyattr, 16)
                pool.wait_ge(s_copy, 96)
            pool.wait_ge(s_tail, 64)
            pool.sem_inc(s_edges, 1)

            def gather_rows(L, first, end):
                with pool.Fori(first, end) as i:
                    for b in range(2):
                        pool.wait_ge(L.s_idx[b], (i + 1) * 16)
                        pool.sem_inc(s_past, 1)
                        for t in range(T):
                            pool.indirect_dma_start(
                                out=gath(L)[:, b, t, :], out_offset=None, in_=L.tab,
                                in_offset=bass.IndirectOffsetOnAxis(ap=idx[:, b, t:t + 1], axis=0)).then_inc(L.s_g[b], 16)

            def layer(L):
                pool.wait_ge(L.s_tabst, 32 if L is L2 else 16)
                if L is L1:
                    gather_rows(L, 0, AHEAD // 2)
                    with pool.If(unsorted):
                        pool.sem_inc(s_edges, 1)
                    with pool.Else():
                        pool.wait_ge(s_copyattr, 16)
                        pool.sem_inc(s_edges, 1)
                    pool.wait_ge(s_dends, 1)
                    pool.wait_ge(s_rowsst, 32)
                    pool.indirect_dma_start(out=col[:, 2:3], out_offset=None, in_=rowend_d,
                                            in_offset=bass.IndirectOffsetOnAxis(ap=dfirst_i[:, :], axis=0)).then_inc(s_ref, 16)
                    pool.wait_ge(L.s_tabst, 32)
                    pool.wait_ge(s_zfill, 16 * sum(L.H for L in LAYERS if L.has_dst))
                if L.has_dst:
                    pool.indirect_dma_start(out=dfv[:, 0:L.H], out_offset=None, in_=L.dnode,
                                            in_offset=bass.IndirectOffsetOnAxis(ap=dfirst_i[:, :], axis=0)).then_inc(L.s_df, 16)
                    with pool.Fori(0, NTB // 2) as i:
                        for b in range(2):
                            pool.wait_ge(L.s_stage, i * 2 + (b + 1))
                            pool.sem_inc(s_past, 1)
                            for t in range(TB):
                                pool.indirect_dma_start(
                                    out=L.dput, out_offset=bass.IndirectOffsetOnAxis(ap=nidx[:, b, t:t + 1], axis=0),
                                    in_=nval[:, b, t * L.H:(t + 1) * L.H], in_offset=None,
                                    bounds_check=EP - 1, oob_is_err=False).then_inc(L.s_scat[b], 16)
                gather_rows(L, AHEAD // 2 if L is L1 else 0, NCH // 2)
                for b in range(2):
                    pool.wait_ge(L.s_st[b], 16 * (NCH // 2 + 1))
                pool.indirect_dma_start(out=frow[:, 0:L.W], out_offset=None, in_=L.scan,
                                        in_offset=bass.IndirectOffsetOnAxis(ap=fix_i[:, :], axis=0),
                                        bounds_check=EP - 1, oob_is_err=False).then_inc(L.s_fr, 16)
                pool.wait_ge(L.s_mend, 1)
                pool.indirect_dma_start(out=L.scan, out_offset=bass.IndirectOffsetOnAxis(ap=fix_i[:, :], axis=0),
                                        in_=frow[:, 0:L.W], in_offset=None,
                                        bounds_check=EP - 1, oob_is_err=False).then_inc(L.s_fr, 16)
                pool.wait_ge(L.s_fr, 32)
                with pool.Fori(0, NTB // 2) as i:
                    for b in range(2):
                        pool.wait_ge(L.s_ni, i * 2 + (b + 1))
                        pool.wait_ge(L.s_nf, i * 2 + (b + 1))
                        pool.sem_inc(s_past, 1)
                        for t in range(TB):
                            pool.indirect_dma_start(
                                out=nrow[:, b, t * L.W:(t + 1) * L.W], out_offset=None, in_=L.scan,
                                in_offset=bass.IndirectOffsetOnAxis(ap=nidx[:, b, t:t + 1], axis=0)).then_inc(L.s_ng[b], 16)

            for L in LAYERS:
                layer(L)

        @block.scalar
        def _(act):
            asked = [0]

            def answer(a, func=ACT.Exp):
                asked[0] += 1
                act.wait_ge(s_exq, asked[0])
                nc.scalar.activation(a, a, func).then_inc(s_exd, 1)

            def start_stores(L):
                for b in range(2):
                    act.wait_ge(L.s_rows, 2)
                    act.dma_start(edges(L.scan)[:, b * T * L.W:(b + 1) * T * L.W],
                                  rows_of(L)[:, b, :, :].rearrange("p t f -> p (t f)")).then_inc(L.s_st[b], 16)

            def edge_loop_spilled():
                def inputs(b, i):
                    act.wait_ge(s_spill[b], (i + 1) * 16)
                    for o, a, w in ((dput, L1.dput, T * H1), (attr, e_attr, T * FEAT), (gin, spill, T * L1.table)):
                        act.dma_start(o[:, b, :], edges(a)[:, bass.ds((i * 2 + b) * w, w)]).then_inc(L1.s_in[b], 16)

                def chunk(b, i, more):
                    act.wait_ge(L1.s_e, i * 2 + (b + 1))
                    nc.scalar.activation(ex[:, :, :], ex[:, :, :], ACT.Exp).then_inc(L1.s_ed, 1)
                    if more:
                        inputs(1 - b, i + b)
                    act.wait_ge(L1.s_rows, i * 2 + (b + 3))
                    act.dma_start(edges(L1.scan)[:, bass.ds((i * 2 + b) * (T * L1.W), T * L1.W)],
                                  rows_of(L1)[:, b, :, :].rearrange("p t f -> p (t f)")).then_inc(L1.s_st[b], 16)

                start_stores(L1)
                inputs(0, 0)
                with act.Fori(0, NCH // 2 - 1) as i:
                    for b in range(2):
                        chunk(b, i, True)
                chunk(0, NCH // 2 - 1, True)
                chunk(1, NCH // 2 - 1, False)

            def edge_loop(L):
                start_stores(L)
                with act.Fori(0, NCH // 2) as i:
                    for b in range(2):
                        if L is L2:
                            act.wait_ge(L.s_e, i * 2 + (b + 1))
                            nc.scalar.activation(ex[:, :, 0:T * L.H], ex[:, :, 0:T * L.H], ACT.Exp).then_inc(L.s_ed, 1)
                        if L is L3:
                            act.wait_ge(L.s_in[b], (i + 1) * 16)
                            nc.scalar.copy(typ_f[:, :], typ[:, b, :]).then_inc(s_tyf, 1)
                            act.wait_ge(s_tyt, i * 2 + (b + 1))
                            nc.scalar.copy(typT[:, :], ps[0:T, 2, 0:P]).then_inc(s_tyc, 1)
                        act.wait_ge(L.s_rows, i * 2 + (b + 3))
                        act.dma_start(edges(L.scan)[:, bass.ds((i * 2 + b) * (T * L.W), T * L.W)],
                                      rows_of(L)[:, b, :, :].rearrange("p t f -> p (t f)")).then_inc(L.s_st[b], 16)

            def node_indices(L):
                act.wait_ge(L.s_fr, 32)
                for b in range(2):
                    nc.scalar.copy(nidx[:, b, :], re_idx[:, b * TB:(b + 1) * TB]).then_inc(L.s_ni, 1)
                with act.Fori(1, NTB // 2) as i:
                    for b in range(2):
                        act.wait_ge(L.s_ng[b], i * (16 * TB))
                        nc.scalar.copy(nidx[:, b, :], re_idx[:, bass.ds((i * 2 + b) * TB, TB)]).then_inc(L.s_ni, 1)

            def node_stage(L):
                exps = [nex[:, 0:2 * TP * L.H]] if L is L1 else [nex[:, 0:2 * TP], selu_e]

                def exponentials(i):
                    for n, a in enumerate(exps):
                        act.wait_ge(L.s_e, i * len(exps) + (NCH + n + 1))
                        nc.scalar.activation(a, a, ACT.Exp).then_inc(L.s_ed, 1)

                def indices(i):
                    for b in range(2):
                        act.wait_ge(L.s_ng[b], (i + 1) * (16 * TB))
                        nc.scalar.copy(nidx[:, b, :], re_idx[:, bass.ds((i * 2 + (b + 2)) * TB, TB)]).then_inc(L.s_ni, 1)

                def mlp_turned(i):
                    for b in range(2):
                        act.wait_ge(s_mpe, i * 6 + (b + 1))
                        nc.scalar.copy(aT[b][0:AH, :], ps_turn[b][0:AH, :]).then_inc(s_mc, 1)

                def mlp_hidden(i):
                    for b in range(2):
                        act.wait_ge(s_mpe, i * 6 + (b + 3))
                        nc.scalar.activation(hT[b][0:HC1, 0, :], ps_turn[b][0:HC1, :], ACT.Exp, bias=b1c[:, 0:1])
                        nc.scalar.activation(hT[b][0:HC1, 1, :], ps_turn[b][0:HC1, :], ACT.Relu, bias=b1c[:, 1:2],
                                             scale=LAM).then_inc(s_ma, 1)

                act.wait_ge(L.s_fr, 32)
                for b in range(2):
                    nc.scalar.copy(nidx[:, b, :], re_idx[:, b * TB:(b + 1) * TB]).then_inc(L.s_ni, 1)
                last = NTB // 2 - 1
                if L is L1:
                    indices(0)
                    exponentials(0)
                    with act.Fori(1, last) as i:
                        mlp_turned(i - 1)
                        indices(i)
                        exponentials(i)
                        mlp_hidden(i - 1)
                    mlp_turned(last - 1)
                    exponentials(last)
                    mlp_hidden(last - 1)
                    mlp_turned(last)
                    mlp_hidden(last)
                else:
                    with act.Fori(0, last) as i:
                        indices(i)
                        exponentials(i)
                    exponentials(last)

            def linear(s, width):
                with act.Fori(0, NTB // 2) as i:
                    for b in range(2):
                        act.wait_ge(s[0], i * 4 + (b + 1))
                        for n, (_, cn) in enumerate(groups(width)):
                            cp = nc.scalar.copy(aT[b][0:cn * width, n * P:(n + 1) * P], ps_turn[b][0:cn * width, n * P:(n + 1) * P])
                        cp.then_inc(s[1], 1)

            def mend(L):
                for _ in range(L.H):
                    answer(sq2[:, :])
                answer(fx[:, 0:2 * L.H])

            answer(nt[:, 0, :], ACT.Sqrt)
            act.wait_ge(s_wm, 1)
            nc.scalar.copy(wm[0:R, :], ps[0:R, 3, 0:M2]).then_inc(s_wmc, 1)

            act.wait_ge(s_wmc, 1)
            act.wait_ge(s_zero, 1)
            act.dma_start(wrel_d.rearrange("(a r) o -> r a o", a=FEAT),
                         wm[0:R, :].rearrange("r (a o) -> r a o", a=FEAT)).then_inc(s_wrl, 16)
            act.wait_ge(s_wrl, 16)
            act.dma_start(wr[0:R, 0, :], wrel_d.rearrange("(r i) o -> r (i o)", i=FEAT)).then_inc(s_wrl, 16)
            act.wait_ge(s_rows, 1)
            act.dma_start(nodes(rowend_d), re[:, :]).then_inc(s_rowsst, 16)
            act.dma_start(nodes(next_slot), rs[:, :]).then_inc(s_rowsst, 16)
            act.wait_ge(s_edges, 1)
            act.dma_start(dst_i, edges(e_dst)).then_inc(s_dstre, 16)
            act.wait_ge(s_dends, 2)
            act.dma_start(dlast_d, col[:, 1:2]).then_inc(s_dlb, 16)
            act.wait_ge(s_dlb, 16)
            act.dma_start(sq1[:, :], dlast_d.rearrange("q o -> (q o)").partition_broadcast(P)).then_inc(s_dlb, 16)

            act.wait_ge(L1.s_df, 16)
            for b in range(2):
                act.wait_ge(L1.s_scat[b], 16 * TB * (NTB // 2))
            act.dma_start(edges(L1.dput)[:, 0:H1], dfv[:, 0:H1]).then_inc(L1.s_dput, 16)
            act.wait_ge(L1.s_dput, 16)
            act.wait_ge(s_edges, 2)
            edge_loop_spilled()
            mend(L1)
            node_stage(L1)
            edge_loop(L2)
            mend(L2)
            node_stage(L2)
            linear(lin["head"], C2)
            answer(nt[:, 0, :], ACT.Sqrt)
            edge_loop(L3)
            node_indices(L3)
            answer(nt[:, 0, :], ACT.Sqrt)
            answer(nt[:, 0, :], ACT.Sqrt)
            linear(lin["gcnw"], FEAT)
            edge_loop(L4)
            node_indices(L4)

        @block.tensor
        def _(pe):
            pe.wait_ge(s_w, 16 * WLOADS)
            nc.tensor.matmul(ps[0:R, 3, 0:M2], wct[:, :], Vs[:, :], start=True, stop=True).then_inc(s_wm, 1)
            pe.wait_ge(s_arena, 1)
            for _ in range(2):
                nc.tensor.matmul(ps[:, 0, 0:K], arena[:, 0:P], arena[:, P:P + K], start=True, stop=False,
                                 skip_group_check=True).then_inc(s_hist, 1)
            oA = oneA.rearrange("p (b t q) -> p b t q", b=2, t=TH)
            oB = oneB.rearrange("p (b t k) -> p b t k", b=2, t=TH)
            with pe.Fori(0, C // TH // 2) as i:
                for b in range(2):
                    pe.wait_ge(s_onehot, i * 2 + (b + 1))
                    for t in range(TH):
                        mm = nc.tensor.matmul(ps[:, 0, 0:K], oA[:, b, t, :], oB[:, b, t, :], start=False, stop=False,
                                              skip_group_check=True)
                    mm.then_inc(s_hist, 1)
            pe.wait_ge(s_onehot, C // TH + 1)
            nc.tensor.matmul(ps[:, 1, 0:1], lower[:, :], col[:, 0:1], start=True, stop=True).then_inc(s_hist, 1)

            def turn(b, width):
                for j in range(TB):
                    mm = nc.tensor.transpose(ps_turn[b][0:width, j * P:(j + 1) * P], stg[b][:, j * width:(j + 1) * width],
                                             ident[:, :])
                return mm

            def linear(s, width, w):
                with pe.Fori(0, NTB // 2) as i:
                    for b in range(2):
                        pe.wait_ge(s[2], i * 4 + (b + 1))
                        pe.sem_inc(s_pe_past, 1)
                        for n, (c0, cn) in enumerate(groups(width)):
                            mm = nc.tensor.transpose(ps_turn[b][0:cn * width, n * P:(n + 1) * P],
                                                     stg[b][:, c0 * width:(c0 + cn) * width], ident[:, :])
                        mm.then_inc(s[0], 1)
                    for b in range(2):
                        pe.wait_ge(s[1], i * 2 + (b + 1))
                        for n, (c0, cn) in enumerate(groups(width)):
                            mm = nc.tensor.matmul(ps_out[b][:, c0 * FEAT:(c0 + cn) * FEAT], aT[b][0:cn * width, n * P:(n + 1) * P],
                                                  w[0:cn * width, 0:cn * FEAT], start=True, stop=True)
                        mm.then_inc(s[0], 1)

            with pe.Fori(0, NTB // 2) as i:
                for b in range(2):
                    pe.wait_ge(s_ms, i * 4 + (b + 1))
                    pe.sem_inc(s_pe_past, 1)
                    turn(b, AH).then_inc(s_mpe, 1)
                for b in range(2):
                    pe.wait_ge(s_mc, i * 2 + (b + 1))
                    for c in range(0, TB * P, 512):
                        mm = nc.tensor.matmul(ps_turn[b][0:HC1, c:min(c + 512, TB * P)], W1bd[:, :],
                                              aT[b][0:AH, c:min(c + 512, TB * P)], start=True, stop=True)
                    mm.then_inc(s_mpe, 1)
                for b in range(2):
                    pe.wait_ge(s_ms, i * 4 + (b + 3))
                    for j in range(TB):
                        mm = nc.tensor.matmul(ps_out[b][:, j * (C2 + 2):(j + 1) * (C2 + 2)], hT[b][0:HC1, 0, j * P:(j + 1) * P],
                                              W2e[:, :], start=True, stop=True)
                    mm.then_inc(s_mpe, 1)
            linear(lin["head"], C2, Wf_bd)

            sel3 = sel.rearrange("k (t r) -> k t r", t=T)

            def spread(g):
                for j in range(4):
                    mm = nc.tensor.matmul(ps[:, g % 2, j * P:(j + 1) * P], sel3[0:T, (g % G4) * 4 + j, :], typT[:, :],
                                          start=True, stop=True)
                mm.then_inc(s_B, 1)

            pe.wait_ge(s_ready, 1)
            with pe.Fori(0, NCH // 2) as i:
                for b in range(2):
                    pe.wait_ge(s_tyf, i * 2 + (b + 1))
                    pe.sem_inc(s_pe_past, 1)
                    nc.tensor.transpose(ps[0:T, 2, 0:P], typ_f[:, :], ident[:, :]).then_inc(s_tyt, 1)
                    pe.wait_ge(s_tyc, i * 2 + (b + 1))
                    spread(b * G4)
                    for g in range(b * G4, (b + 1) * G4):
                        if g + 1 < (b + 1) * G4:
                            spread(g + 1)
                        pe.wait_ge(s_oh, i * (2 * G4) + (g + 1))
                        pe.wait_ge(s_wfree, i * (2 * G4) + (g + 1))
                        for j in range(4):
                            for part in range(3):
                                mm = nc.tensor.matmul(
                                    ps[:, 4 + 2 * (g % 2) + j // 2, (j % 2) * M2:(j % 2 + 1) * M2],
                                    oh[:, g % 2, j * P:(j + 1) * P], wsp[:, part, :], start=(part == 0), stop=(part == 2))
                        mm.then_inc(s_Wr, 1)
            linear(lin["gcnw"], FEAT, W3_bd)

        @block.vector
        def _(dve):
            v = nc.vector
            count = [0, 0]

            def link(ins):
                count[0] += 1
                ins.then_inc(s_v, 1)
                dve.wait_ge(s_v, count[0])

            def ask(ins):
                count[1] += 1
                ins.then_inc(s_exq, 1)
                dve.wait_ge(s_exd, count[1])

            def leaky(o, a):
                return v.scalar_tensor_tensor(out=o, in0=a, scalar=SLOPE, in1=a, op0=ALU.mult, op1=ALU.max)

            v.memset(dst_i[:, ELAST:C], N)
            v.memset(nxt[:, :], N)
            v.memset(xs[:, NLAST * FEAT:], 0.0)
            v.memset(Wf_bd[:, :], 0.0)
            v.memset(W3_bd[:, :], 0.0)
            v.memset(W1bd[:, :], 0.0).then_inc(s_pad, 1)
            for L in LAYERS:
                dve.sem_inc(L.s_nf, 2)
            dve.sem_inc(s_wfree, 2)
            v.memset(dsc[:, :, :], 0.0)
            v.memset(emax[:, :], 0.0)
            v.memset(frow[:, :], 0.0)
            v.memset(wr[:, :, :], 0.0).then_inc(s_zero, 1)
            dve.wait_ge(s_zero, 1)

            dve.wait_ge(s_iota, 2)
            v.tensor_copy(iq[:, :], iq_i[:, :])
            v.tensor_copy(iqb[:, :], iq_i[:, :])
            link(v.tensor_copy(ip[:, :], ip_i[:, :]))
            v.tensor_scalar(ident[:, :], iq[:, :], ip[:, 0:1], None, ALU.is_equal)
            v.tensor_scalar(lower[:, :], iq[:, :], ip[:, 0:1], None, ALU.is_gt)
            link(v.tensor_scalar(mask[:, :], iq[:, :], ip[:, 0:1], None, ALU.is_lt))

            dve.wait_ge(s_dst_in, 48)
            v.tensor_copy(col[:, 3:4], nxt[:, :])
            link(v.tensor_copy(dst_f[:, :], dst_i))
            v.tensor_tensor(notb[:, 1:C], dst_f[:, 0:C - 1], dst_f[:, 1:C], ALU.is_gt)
            link(v.tensor_tensor(notb[:, 0:1], dst_f[:, C - 1:C], col[:, 3:4], ALU.is_gt))
            v.tensor_reduce(flag[:, 0:1], notb[:, :], AX_X, ALU.max).then_inc(s_viol, 1)

            dve.wait_ge(s_w, 16 * WLOADS)
            w1t = scanbuf[:, FEAT * HC1:2 * FEAT * HC1]
            for q in range(2):
                link(v.tensor_tensor(w1t.rearrange("p (i c) -> p i c", i=FEAT), W1b.rearrange("p (i c) -> p i c", i=FEAT),
                                     bc(as1[:, q, :].unsqueeze(1), [P, FEAT, HC1]), ALU.mult))
                link(v.tensor_reduce(ws1[:, q, :].rearrange("p (h i) -> p i h", h=H1),
                                     w1t.rearrange("p (i h c) -> p i h c", i=FEAT, h=H1), AX_X, ALU.add))

            def layernorm_relu():
                link(v.tensor_reduce(nt[:, 1, :], xs3, AX_X, ALU.add))
                link(v.tensor_scalar(nt[:, 1, :], nt[:, 1, :], 1.0 / FEAT, None, ALU.mult))
                link(v.tensor_tensor(hs3, xs3, bc(nt[:, 1, :].unsqueeze(2), [P, K, FEAT]), ALU.subtract))
                link(v.tensor_tensor(tab3(FEAT), hs3, hs3, ALU.mult))
                link(v.tensor_reduce(nt[:, 0, :], tab3(FEAT), AX_X, ALU.add))
                ask(v.tensor_scalar(nt[:, 0, :], nt[:, 0, :], 1.0 / FEAT, 1e-5, ALU.mult, ALU.add))
                link(v.reciprocal(nt[:, 0, :], nt[:, 0, :]))
                link(v.tensor_tensor(hs3, hs3, bc(nt[:, 0, :].unsqueeze(2), [P, K, FEAT]), ALU.mult))
                link(v.tensor_scalar(hs[:, :], hs[:, :], 0.0, None, ALU.max))

            def project(o, w, heads):
                tmp = scanbuf[:, 0:K * heads * FEAT].rearrange("p (k h i) -> p k h i", k=K, h=heads)
                link(v.tensor_tensor(tmp, bc(hs3.unsqueeze(2), [P, K, heads, FEAT]),
                                     bc(w.rearrange("p (h i) -> p h i", h=heads).unsqueeze(1), [P, K, heads, FEAT]), ALU.mult))
                link(v.tensor_reduce(o, tmp, AX_X, ALU.add))

            dve.wait_ge(s_x, 32)
            layernorm_relu()
            project(kh(snode, H1), ws1[:, 0, :], H1)
            v.tensor_copy(tab3(L1.table)[:, :, 0:FEAT], hs3)
            v.tensor_copy(tab3(L1.table)[:, :, FEAT:], kh(snode, H1)).then_inc(L1.s_tab, 1)
            project(kh(dnode, H1), ws1[:, 1, :], H1)
            dve.sem_inc(L1.s_tab, 1)
            v.tensor_scalar(b1c[:, 1:2], b1c[:, 0:1], LAM, None, ALU.mult)
            link(v.tensor_tensor(t2[:, :, :], bc(W2e[:, 0:C2].unsqueeze(1), [HC1, 2, C2]), as2[:, :, :], ALU.mult))
            link(v.tensor_reduce(W2e[:, C2:C2 + 2], t2[:, :, :], AX_X, ALU.add))
            for q in range(3):
                link(v.tensor_tensor(wvt[:, :].rearrange("p (o i) -> p o i", o=FEAT),
                                     Wsb[:, :].rearrange("p (o i) -> p o i", o=FEAT),
                                     bc(Wab[:, q * FEAT:(q + 1) * FEAT].unsqueeze(2), [P, FEAT, FEAT]), ALU.mult))
                link(v.tensor_reduce(wv[:, q, :], wvt[:, :].rearrange("p (o i) -> p i o", o=FEAT), AX_X, ALU.add))

            oA = oneA.rearrange("p (b t q) -> p b t q", b=2, t=TH)
            oB = oneB.rearrange("p (b t k) -> p b t k", b=2, t=TH)
            s_hist_chain = sem("hist_chain")
            hist_steps = 4
            with dve.Fori(0, C // TH // 2) as i:
                for b in range(2):
                    base = i * (2 * hist_steps) + b * hist_steps
                    d = dst_f[:, bass.ds((i * 2 + b) * TH, TH)]
                    v.tensor_scalar(hd[:, 0, :], d, 1.0 / K, 0.5 / K - 0.5, ALU.mult, ALU.add).then_inc(s_hist_chain, 1)
                    dve.wait_ge(s_hist_chain, base + 1)
                    v.tensor_scalar(hd[:, 1, :], hd[:, 0, :], RNE, None, ALU.add).then_inc(s_hist_chain, 1)
                    dve.wait_ge(s_hist_chain, base + 2)
                    v.tensor_scalar(hd[:, 2, :], hd[:, 1, :], RNE, None, ALU.subtract).then_inc(s_hist_chain, 1)
                    dve.wait_ge(s_hist_chain, base + 3)
                    v.scalar_tensor_tensor(out=hd[:, 3, :], in0=hd[:, 2, :], scalar=-float(K), in1=d,
                                           op0=ALU.mult, op1=ALU.add).then_inc(s_hist_chain, 1)
                    dve.wait_ge(s_hist, i * 2 + (b + 1))
                    v.tensor_tensor(oA[:, b, :, :], bc(iqb[:, :].unsqueeze(1), [P, TH, P]),
                                    bc(hd[:, 2, :].unsqueeze(2), [P, TH, P]), ALU.is_equal)
                    dve.wait_ge(s_hist_chain, base + 4)
                    v.tensor_tensor(oB[:, b, :, :], bc(iqb[:, 0:K].unsqueeze(1), [P, TH, K]),
                                    bc(hd[:, 3, :].unsqueeze(2), [P, TH, K]), ALU.is_equal).then_inc(s_onehot, 1)
            dve.wait_ge(s_hist, C // TH + 2)

            v.memset(nt[:, 1, :], 1.0)
            link(v.tensor_copy(cnt[:, :], ps[:, 0, 0:K]))
            link(v.tensor_tensor_scan(re[:, :], nt[:, 1, :], cnt[:, :], 0.0, ALU.mult, ALU.add))
            v.tensor_copy(col[:, 0:1], re[:, K - 1:K]).then_inc(s_onehot, 1)
            dve.wait_ge(s_hist, C // TH + 3)
            link(v.tensor_scalar(re[:, :], re[:, :], ps[:, 1, 0:1], None, ALU.add))
            v.tensor_scalar(has[:, :], cnt[:, :], 1.0, None, ALU.min)
            link(v.tensor_tensor(rs[:, :], re[:, :], cnt[:, :], ALU.subtract))
            v.tensor_scalar(re_idx[:, :], re[:, :], -1.0, 0.0, ALU.add, ALU.max)
            link(v.tensor_scalar(nt[:, 0, :], has[:, :], -SKIP, SKIP, ALU.mult, ALU.add))
            v.tensor_tensor(rs_idx[:, :], nt[:, 0, :], rs[:, :], ALU.add).then_inc(s_rows, 1)

            dve.wait_ge(s_dstre, 16)
            link(v.tensor_copy(dst_f[:, :], dst_i))
            v.tensor_tensor(notb[:, 1:C], dst_f[:, 1:C], dst_f[:, 0:C - 1], ALU.is_equal)
            v.memset(notb[:, 0:1], 0.0)
            v.tensor_copy(dfirst_i[:, :], dst_i[:, 0:1]).then_inc(s_dends, 1)
            v.tensor_copy(col[:, 1:2], dst_f[:, C - 1:C]).then_inc(s_dends, 1)
            dve.wait_ge(s_dlb, 32)
            link(v.tensor_scalar(sq2[:, :], sq1[:, :], dst_f[:, 0:1], None, ALU.is_equal))
            link(v.tensor_tensor(mask[:, :], mask[:, :], sq2[:, :], ALU.mult))
            v.tensor_scalar(negmask[:, :], mask[:, :], 1.0, BIG, ALU.subtract, ALU.mult)
            link(v.tensor_reduce(col[:, 4:5], mask[:, :], AX_X, ALU.max))
            dve.wait_ge(s_ref, 16)
            link(v.tensor_scalar(col[:, 5:6], ip[:, :], float(C), float(C), ALU.mult, ALU.add))
            link(v.tensor_tensor(col[:, 6:7], col[:, 2:3], col[:, 5:6], ALU.is_le))
            link(v.tensor_tensor(col[:, 6:7], col[:, 6:7], col[:, 4:5], ALU.mult))
            link(v.tensor_scalar(col[:, 6:7], col[:, 6:7], -SKIP, SKIP - 1.0, ALU.mult, ALU.add))
            link(v.tensor_tensor(fix_i[:, :], col[:, 2:3], col[:, 6:7], ALU.add))

            def stage_dst(L):
                w = TB * L.H
                for b in range(2):
                    v.tensor_copy(nval[:, b, 0:w], dnode[:, b * w:(b + 1) * w])
                    v.tensor_copy(nidx[:, b, :], rs_idx[:, b * TB:(b + 1) * TB]).then_inc(L.s_stage, 1)
                with dve.Fori(1, NTB // 2) as i:
                    for b in range(2):
                        dve.wait_ge(L.s_scat[b], i * (16 * TB))
                        v.tensor_copy(nval[:, b, 0:TB * L.H], dnode[:, bass.ds((i * 2 + b) * (TB * L.H), TB * L.H)])
                        v.tensor_copy(nidx[:, b, :], rs_idx[:, bass.ds((i * 2 + b) * TB, TB)]).then_inc(L.s_stage, 1)

            def head(a, L, h, t0=0, t1=T):
                return a.rearrange("p (t h) -> p t h", h=L.H)[:, t0:t1, h]

            def scan(o, keep, add, init, op0=ALU.mult, op1=ALU.add):
                return v.tensor_tensor_scan(o, keep, add, init, op0, op1)

            def edge_loop_attention(L):
                rows = rows_of(L)
                G = gin[:, :, :].rearrange("p b (t f) -> p b t f", t=T) if L is L1 else gath(L)
                H, D = L.H, L.D
                mo, ao = H + H * D, 2 * H + H * D
                g3 = lambda a: a.rearrange("p (t h) -> p t h", h=H)
                X0, X1 = ex[:, 0, 0:T * H], ex[:, 1, 0:T * H]
                em = g3(emax[:, 0:(T + 1) * H])
                acc = ph[:, :, 0:H * D]
                NST = 6 + (L is L1)
                NIN = 48 if L is L1 else 16
                with dve.Fori(0, NCH // 2) as i:
                    for b in range(2):
                        base = i * (2 * NST) + b * NST
                        step = [0]

                        def chain(ins):
                            step[0] += 1
                            ins.then_inc(L.s_chain, 1)
                            dve.wait_ge(L.s_chain, base + step[0])

                        c0 = (i * 2 + b) * T
                        v.tensor_copy(nb[:, :], notb[:, bass.ds(c0, T)])
                        chain(v.tensor_scalar(negb[:, :], notb[:, bass.ds(c0, T)], 1.0, BIG, ALU.subtract, ALU.mult))
                        dve.wait_ge(L.s_in[b], (i + 1) * NIN)
                        if L is not L1:
                            dve.wait_ge(L.s_g[b], (i + 1) * (16 * T))
                        dve.wait_ge(L.s_st[b], (i + 1) * 16)
                        for h in range(H):
                            scan(head(dsc[:, b, 0:T * H], L, h), nb[:, :], head(dput[:, b, 0:T * H], L, h),
                                 head(dsc[:, 1 - b, 0:T * H], L, h, T - 1, T))
                            last = scan(rows[:, b, :, mo + h], negb[:, :], G[:, b, :, D + h],
                                        rows[:, 1 - b, T - 1:T, mo + h], ALU.add, ALU.max)
                        chain(last)
                        v.tensor_tensor(g3(lgt[:, 0, 0:T * H]), G[:, b, :, D:D + H], g3(dsc[:, b, 0:T * H]), ALU.add)
                        chain(v.tensor_tensor(g3(lgt[:, 1, 0:T * H]), rows[:, b, :, mo:mo + H], g3(dsc[:, b, 0:T * H]), ALU.add))
                        leaky(X0, lgt[:, 0, 0:T * H])
                        chain(leaky(emax[:, H:(T + 1) * H], lgt[:, 1, 0:T * H]))
                        v.tensor_tensor(X0, X0, emax[:, H:(T + 1) * H], ALU.subtract)
                        chain(v.tensor_tensor(X1, emax[:, 0:T * H], emax[:, H:(T + 1) * H], ALU.subtract))
                        v.tensor_tensor(g3(X1), g3(X1), bc(negb[:, :].unsqueeze(2), [P, T, H]), ALU.add).then_inc(L.s_e, 1)
                        v.tensor_copy(emax[:, 0:H], emax[:, T * H:(T + 1) * H])
                        if L is L1:
                            at = attr[:, b, :].rearrange("p (t f) -> p t f", f=FEAT)
                            for f in range(FEAT):
                                scan(rows[:, b, :, ao + f], nb[:, :], at[:, :, f], rows[:, 1 - b, T - 1:T, ao + f])
                            tmp = prod[:, 0:T * FEAT].rearrange("p (t f) -> p t f", f=FEAT)
                            chain(v.tensor_tensor(tmp, at, bc(wv[:, 1, :].unsqueeze(1), [P, T, FEAT]), ALU.mult))
                            v.tensor_reduce(tE[:, bass.ds(c0, T)], tmp, AX_X, ALU.add)
                        dve.wait_ge(L.s_ed, i * 2 + (b + 1))
                        chain(v.tensor_tensor(acc.rearrange("p t (h d) -> p t h d", h=H),
                                              bc(G[:, b, :, 0:D].unsqueeze(2), [P, T, H, D]),
                                              bc(g3(X0).unsqueeze(3), [P, T, H, D]), ALU.mult))
                        for h in range(H):
                            scan(rows[:, b, :, h], head(X1, L, h), head(X0, L, h), rows[:, 1 - b, T - 1:T, h])
                            for j in range(D):
                                f = h * D + j
                                last = scan(rows[:, b, :, H + f], head(X1, L, h), acc[:, :, f], rows[:, 1 - b, T - 1:T, H + f])
                        last.then_inc(L.s_rows, 1)
                        dve.wait_ge(L.s_rows, i * 2 + (b + 3))
                        assert step[0] == NST

            def edge_loop_relation(L):
                rows, G = rows_of(L), gath(L)
                msg, wmsg = ph[:, :, FEAT:2 * FEAT], ph[:, :, 0:FEAT]
                NST = 2 + G4
                with dve.Fori(0, NCH // 2) as i:
                    for b in range(2):
                        base = i * (2 * NST) + b * NST
                        step = [0]

                        def chain(ins):
                            step[0] += 1
                            ins.then_inc(L.s_chain, 1)
                            dve.wait_ge(L.s_chain, base + step[0])

                        def onehot(g):
                            dve.wait_ge(s_B, i * (2 * G4) + (g + 1))
                            v.tensor_scalar(oh[:, g % 2, :], ps[:, g % 2, :], ip[:, 0:1], None, ALU.is_equal).then_inc(s_oh, 1)

                        c0 = (i * 2 + b) * T
                        v.tensor_copy(nb[:, :], notb[:, bass.ds(c0, T)])
                        dve.wait_ge(L.s_g[b], (i + 1) * (16 * T))
                        dve.wait_ge(L.s_st[b], (i + 1) * 16)
                        chain(v.tensor_tensor(ef[:, :], G[:, b, :, FEAT], tE[:, bass.ds(c0, T)], ALU.add))
                        onehot(b * G4)
                        for g in range(b * G4, (b + 1) * G4):
                            if g + 1 < (b + 1) * G4:
                                onehot(g + 1)
                            t0 = (g % G4) * 4
                            dve.wait_ge(s_Wr, i * (2 * G4) + (g + 1))
                            dve.wait_ge(s_wfree, i * (2 * G4) + (g + 2))
                            w = ps[:, 4 + 2 * (g % 2):6 + 2 * (g % 2), :].rearrange("p b (t i o) -> p (b t) i o", t=2, i=FEAT)
                            pr = prod[:, :].rearrange("p (t i o) -> p t i o", t=4, i=FEAT)
                            chain(v.tensor_tensor(pr, w, bc(G[:, b, t0:t0 + 4, 0:FEAT].unsqueeze(3), [P, 4, FEAT, FEAT]), ALU.mult))
                            v.tensor_reduce(msg[:, t0:t0 + 4, :], pr.rearrange("p t i o -> p t o i"), AX_X, ALU.add)\
                             .then_inc(s_wfree, 1)
                        dve.wait_ge(s_wfree, i * (2 * G4) + ((b + 1) * G4 + 2))
                        chain(v.tensor_tensor(wmsg, msg, bc(ef[:, :].unsqueeze(2), [P, T, FEAT]), ALU.mult))
                        for f in range(2 * FEAT):
                            last = scan(rows[:, b, :, f], nb[:, :], ph[:, :, f], rows[:, 1 - b, T - 1:T, f])
                        last.then_inc(L.s_rows, 1)
                        dve.wait_ge(L.s_rows, i * 2 + (b + 3))
                        assert step[0] == NST

            def edge_loop_sum(L):
                rows, G = rows_of(L), gath(L)
                with dve.Fori(0, NCH // 2) as i:
                    for b in range(2):
                        v.tensor_copy(nb[:, :], notb[:, bass.ds((i * 2 + b) * T, T)]).then_inc(L.s_chain, 1)
                        dve.wait_ge(L.s_chain, i * 2 + (b + 1))
                        dve.wait_ge(L.s_g[b], (i + 1) * (16 * T))
                        dve.wait_ge(L.s_st[b], (i + 1) * 16)
                        for f in range(FEAT):
                            last = scan(rows[:, b, :, f], nb[:, :], G[:, b, :, f], rows[:, 1 - b, T - 1:T, f])
                        last.then_inc(L.s_rows, 1)
                        dve.wait_ge(L.s_rows, i * 2 + (b + 3))

            def mend_sums(L, c0, c1):
                lr = last_rows(L)[:, :, c0:c1]
                link(v.tensor_tensor(lr, lr, bc(mask[:, :].unsqueeze(2), [P, P, c1 - c0]), ALU.mult))
                link(v.tensor_reduce(crow[:, c0:c1], lr.rearrange("p q f -> p f q"), AX_X, ALU.add))
                dve.wait_ge(L.s_fr, 16)
                link(v.tensor_tensor(frow[:, c0:c1], frow[:, c0:c1], crow[:, c0:c1], ALU.add))

            def mend_attention(L):
                H, D = L.H, L.D
                mo = H + H * D
                lr = last_rows(L)
                F = lambda n, h=None: fx[:, n * H:(n + 1) * H] if h is None else fx[:, n * H + h:n * H + h + 1]
                for h in range(H):
                    link(v.tensor_tensor(sq1[:, :], lr[:, :, mo + h], negmask[:, :], ALU.add))
                    link(v.tensor_reduce(F(2, h), sq1[:, :], AX_X, ALU.max))
                    link(v.tensor_tensor(F(3, h), F(2, h), dfv[:, h:h + 1], ALU.add))
                    link(leaky(F(4, h), F(3, h)))
                    link(v.tensor_scalar(sq1[:, :], lr[:, :, mo + h], dfv[:, h:h + 1], None, ALU.add))
                    link(leaky(sq2[:, :], sq1[:, :]))
                    ask(v.tensor_scalar(sq2[:, :], sq2[:, :], F(4, h), 0.0, ALU.subtract, ALU.min))
                    link(v.tensor_tensor(sq2[:, :], sq2[:, :], mask[:, :], ALU.mult))
                    for c0, c1 in ((h, h + 1), (H + h * D, H + (h + 1) * D)):
                        link(v.tensor_tensor(lr[:, :, c0:c1], lr[:, :, c0:c1], bc(sq2[:, :].unsqueeze(2), [P, P, c1 - c0]), ALU.mult))
                        link(v.tensor_reduce(crow[:, c0:c1], lr[:, :, c0:c1].rearrange("p q f -> p f q"), AX_X, ALU.add))
                dve.wait_ge(L.s_fr, 16)
                fm = frow[:, mo:mo + H]
                link(v.tensor_tensor(F(5), fm, F(2), ALU.max))
                link(v.tensor_tensor(F(3), F(5), dfv[:, 0:H], ALU.add))
                link(leaky(F(6), F(3)))
                link(v.tensor_tensor(F(3), fm, dfv[:, 0:H], ALU.add))
                link(leaky(F(7), F(3)))
                v.tensor_tensor(F(0), F(7), F(6), ALU.subtract)
                ask(v.tensor_tensor(F(1), F(4), F(6), ALU.subtract))
                v.tensor_copy(fm, F(5))
                for r, n in ((frow, 0), (crow, 1)):
                    v.tensor_tensor(r[:, 0:H], r[:, 0:H], F(n), ALU.mult)
                    a = r[:, H:mo].rearrange("p (h d) -> p h d", h=H)
                    last = v.tensor_tensor(a, a, bc(F(n).unsqueeze(2), [P, H, D]), ALU.mult)
                link(last)
                link(v.tensor_tensor(frow[:, 0:mo], frow[:, 0:mo], crow[:, 0:mo], ALU.add))

            def collect(L):
                with dve.Fori(0, NTB // 2) as i:
                    for b in range(2):
                        dve.wait_ge(L.s_ng[b], (i + 1) * (16 * TB))
                        v.tensor_copy(arena[:, bass.ds((i * 2 + b) * (TB * L.W), TB * L.W)], nrow[:, b, 0:TB * L.W])\
                         .then_inc(L.s_nf, 1)
                dve.wait_ge(L.s_nf, NTB + 2)

            def mlp_stage(i):
                for b in range(2):
                    v.tensor_copy(stg[b].rearrange("p (k c) -> p k c", k=TB),
                                  arena[:, bass.ds((i * 2 + b) * (TB * L1.W), TB * L1.W)]
                                  .rearrange("p (k c) -> p k c", k=TB)[:, :, H1:H1 + AH]).then_inc(s_ms, 1)

            def mlp_selu(i):
                for b in range(2):
                    h = hT[b][0:HC1, :, :]
                    dve.wait_ge(s_ma, i * 2 + (b + 1))
                    v.tensor_scalar(h[:, 0, :], h[:, 0, :], 1.0, 1.0, ALU.min, ALU.subtract).then_inc(mlp_chain, 1)
                    dve.wait_ge(mlp_chain, i * 2 + (b + 1))
                    v.scalar_tensor_tensor(out=h[:, 0, :], in0=h[:, 0, :], scalar=LAMALPHA, in1=h[:, 1, :],
                                           op0=ALU.mult, op1=ALU.add).then_inc(s_ms, 1)

            def mlp_result(i):
                for b in range(2):
                    dve.wait_ge(s_mpe, i * 6 + (b + 5))
                    o = ps_out[b][:, 0:TB * (C2 + 2)].rearrange("p (j c) -> p j c", j=TB)
                    v.tensor_copy(tab[:, bass.ds((i * 2 + b) * (TB * (C2 + 1)), TB * (C2 + 1))].rearrange("p (j c) -> p j c", j=TB),
                                  o[:, :, 0:C2 + 1])
                    v.tensor_copy(dnode[:, bass.ds((i * 2 + b) * TB, TB)], o[:, :, C2 + 1]).then_inc(mlp_out, 1)

            def finish_attention(L, edge_steps, rest):
                H, D = L.H, L.D
                mo = H + H * D
                kh7 = lambda a: a.rearrange("p (k h) -> p k h", h=H)
                w = TP * H
                M1, LM = kh7(nm[:, 0:w]), kh7(nm[:, w:2 * w])
                XN, XS = kh7(nex[:, 0:w]), kh7(nex[:, w:2 * w])
                asks = 1 if L is L1 else 2
                link(v.tensor_scalar(nt[:, 0, :], has[:, :], 1.0, BIG, ALU.subtract, ALU.mult))
                if L is L1:
                    link(v.tensor_scalar(nt[:, 1, :], cnt[:, :], 1.0, None, ALU.max))
                    link(v.reciprocal(nt[:, 1, :], nt[:, 1, :]))
                    link(v.tensor_tensor(nt[:, 1, :], nt[:, 1, :], has[:, :], ALU.mult))
                steps = 10 + 4 * H + (2 if L is L1 else 3)

                def pair(i):
                    base = i * steps + NCH * edge_steps
                    step, asked = [0], [0]

                    def chain(ins):
                        step[0] += 1
                        ins.then_inc(L.s_chain, 1)
                        dve.wait_ge(L.s_chain, base + step[0])

                    def ask_chunk(ins):
                        asked[0] += 1
                        ins.then_inc(L.s_e, 1)
                        dve.wait_ge(L.s_ed, i * asks + (NCH + asked[0]))

                    cols = lambda a, c: a[:, bass.ds(i * (TP * c), TP * c)]
                    A = cols(arena, L.W).rearrange("p (k f) -> p k f", k=TP)
                    s, d = kh7(cols(snode, H)), kh7(cols(dnode, H))
                    big = cols(nt[:, 0, :], 1).unsqueeze(2)
                    for b in range(2):
                        dve.wait_ge(L.s_ng[b], (i + 1) * (16 * TB))
                        v.tensor_copy(arena[:, bass.ds((i * 2 + b) * (TB * L.W), TB * L.W)], nrow[:, b, 0:TB * L.W])\
                         .then_inc(L.s_nf, 1)
                    dve.wait_ge(L.s_nf, i * 2 + 4)
                    m = A[:, :, mo:mo + H]
                    chain(v.tensor_tensor(m, m, bc(big, [P, TP, H]), ALU.add))
                    chain(v.tensor_tensor(M1, m, s, ALU.max))
                    chain(v.tensor_tensor(M1, M1, d, ALU.add))
                    chain(leaky(LM, M1))
                    v.tensor_tensor(XN, m, d, ALU.add)
                    chain(v.tensor_tensor(M1, s, d, ALU.add))
                    leaky(XN, XN)
                    chain(leaky(XS, M1))
                    v.tensor_tensor(XN, XN, LM, ALU.subtract)
                    ask_chunk(v.tensor_tensor(XS, XS, LM, ALU.subtract))
                    z = A[:, :, 0:H]
                    chain(v.tensor_tensor(z, z, XN, ALU.mult))
                    chain(v.tensor_tensor(z, z, XS, ALU.add))
                    chain(v.tensor_scalar(LM, z, 1e-16, None, ALU.add))
                    chain(v.reciprocal(nm[:, 0:w], nm[:, w:2 * w]))
                    own = cols(hs, FEAT) if L is L1 else cols(tab, L2.table)
                    own = own.rearrange("p (k f) -> p k f", k=TP)[:, :, 0:D]
                    t0 = 0 if L is L1 else K * C2
                    t = scanbuf[:, t0:t0 + TP * D].rearrange("p (k d) -> p k d", d=D)
                    for h in range(H):
                        a = A[:, :, H + h * D:H + (h + 1) * D]
                        chain(v.tensor_tensor(a, a, bc(XN[:, :, h:h + 1], [P, TP, D]), ALU.mult))
                        chain(v.tensor_tensor(t, own, bc(XS[:, :, h:h + 1], [P, TP, D]), ALU.mult))
                        chain(v.tensor_tensor(a, a, t, ALU.add))
                        chain(v.tensor_tensor(a, a, bc(M1[:, :, h:h + 1], [P, TP, D]), ALU.mult))
                    rest(A, cols, chain, ask_chunk)
                    assert step[0] == steps and asked[0] == asks, step

                if L is L1:
                    pair(0)
                    mlp_stage(0)
                    with dve.Fori(1, NTB // 2) as i:
                        pair(i)
                        mlp_selu(i - 1)
                        mlp_stage(i)
                        mlp_result(i - 1)
                    mlp_selu(NTB // 2 - 1)
                    mlp_result(NTB // 2 - 1)
                else:
                    with dve.Fori(0, NTB // 2) as i:
                        pair(i)

            def linear(s, src, width, out2):
                with dve.Fori(0, NTB // 2) as i:
                    for b in range(2):
                        v.tensor_copy(stg[b][:, 0:TB * width], src[:, bass.ds((i * 2 + b) * (TB * width), TB * width)])\
                         .then_inc(s[2], 1)
                    for b in range(2):
                        dve.wait_ge(s[0], i * 4 + (b + 3))
                        v.tensor_copy(out2[:, bass.ds((i * 2 + b) * (TB * FEAT), TB * FEAT)], ps_out[b][:, 0:TB * FEAT])\
                         .then_inc(s[2], 1)
                dve.wait_ge(s[2], 2 * NTB)

            link(v.memset(scanbuf[:, :], 0.0))
            dve.sem_inc(L1.s_rows, 2)
            stage_dst(L1)
            edge_loop_attention(L1)
            dve.wait_ge(L1.s_last, 32)
            mend_attention(L1)
            mend_sums(L1, L1.W - FEAT, L1.W)
            dve.sem_inc(L1.s_mend, 1)

            def edge_mean(A, cols, chain, ask_chunk):
                am = A[:, :, L1.W - FEAT:]
                xk = cols(xs, FEAT).rearrange("p (k f) -> p k f", k=TP)
                chain(v.tensor_tensor(am, am, bc(cols(nt[:, 1, :], 1).unsqueeze(2), [P, TP, FEAT]), ALU.mult))
                chain(v.tensor_tensor(xk, xk, am, ALU.add))

            finish_attention(L1, 7, edge_mean)
            dve.wait_ge(mlp_out, NTB)

            link(v.tensor_copy(kh(snode, 1), tab3(L2.table)[:, :, C2:C2 + 1]))
            dve.sem_inc(L2.s_tab, 1)
            link(v.memset(scanbuf[:, 0:2 * T * L2.W], 0.0))
            dve.sem_inc(L2.s_rows, 2)
            v.memset(dsc[:, :, :], 0.0)
            link(v.memset(emax[:, :], 0.0))
            stage_dst(L2)
            edge_loop_attention(L2)
            dve.wait_ge(L2.s_last, 32)
            mend_attention(L2)
            dve.sem_inc(L2.s_mend, 1)

            def selu(A, cols, chain, ask_chunk):
                u = A[:, :, 1:1 + C2]
                e, r = selu_e[:, :], selu_r[:, :]
                in_k = lambda a: a.rearrange("p (k c) -> p k c", c=C2)
                chain(v.tensor_tensor(u, u, bc(b2b[:, :].unsqueeze(1), [P, TP, C2]), ALU.add))
                v.tensor_scalar(in_k(r), u, LAM, 0.0, ALU.mult, ALU.max)
                ask_chunk(v.tensor_copy(in_k(e), u))
                chain(v.tensor_scalar(e, e, 1.0, 1.0, ALU.min, ALU.subtract))
                chain(v.scalar_tensor_tensor(out=cols(scanbuf, C2), in0=e, scalar=LAMALPHA, in1=r, op0=ALU.mult, op1=ALU.add))

            finish_attention(L2, 6, selu)
            linear(lin["head"], scanbuf, C2, hs)
            link(v.tensor_tensor(xs3, xs3, hs3, ALU.add))
            link(v.tensor_tensor(xs3, xs3, bc(bfb[:, :].unsqueeze(1), [P, K, FEAT]), ALU.add))

            layernorm_relu()
            project(kh(snode, 1), wv[:, 0, :], 1)
            project(kh(dnode, 1), wv[:, 2, :], 1)
            v.tensor_copy(tab3(L3.table)[:, :, 0:FEAT], hs3)
            v.tensor_copy(tab3(L3.table)[:, :, FEAT:], kh(snode, 1)).then_inc(L3.s_tab, 1)
            dve.wait_ge(s_wrl, 32)
            link(v.tensor_copy(wsp[:, 0, :], wr[:, 0, :]))
            for part in (1, 2):
                link(v.tensor_tensor(wr[:, 0, :], wr[:, 0, :], wsp[:, part - 1, :], ALU.subtract))
                link(v.tensor_copy(wsp[:, part, :], wr[:, 0, :]))
            link(v.memset(scanbuf[:, 0:2 * T * L3.W], 0.0))
            dve.sem_inc(L3.s_rows, 2)
            link(v.tensor_scalar(sel[0:T, :].rearrange("k (t r) -> k t r", t=T),
                                 bc(iq[0:T, 0:T].unsqueeze(2), [T, T, P]), ip[0:T, 0:1], None, ALU.is_equal))
            dve.sem_inc(s_ready, 1)
            edge_loop_relation(L3)
            dve.wait_ge(L3.s_last, 32)
            mend_sums(L3, 0, 2 * FEAT)
            dve.sem_inc(L3.s_mend, 1)
            collect(L3)

            def add_sums(L, scale):
                a = node_rows(L)[:, :, 0:FEAT]
                link(v.tensor_tensor(a, a, bc(scale.unsqueeze(2), [P, K, FEAT]), ALU.mult))
                link(v.tensor_tensor(xs3, xs3, a, ALU.add))

            a3, m3 = node_rows(L3)[:, :, 0:FEAT], node_rows(L3)[:, :, FEAT:]
            link(v.tensor_tensor(m3, m3, bc(dnode[:, 0:K].unsqueeze(2), [P, K, FEAT]), ALU.mult))
            link(v.tensor_tensor(a3, a3, m3, ALU.add))
            add_sums(L3, has[:, :])

            layernorm_relu()
            ask(v.tensor_scalar(nt[:, 0, :], cnt[:, :], 1.0, None, ALU.add))
            link(v.reciprocal(nt[:, 1, :], nt[:, 0, :]))
            linear(lin["gcnw"], hs, FEAT, tab)
            v.tensor_tensor(tab3(FEAT), tab3(FEAT), bc(nt[:, 1, :].unsqueeze(2), [P, K, FEAT]), ALU.mult).then_inc(L4.s_tab, 1)
            link(v.memset(scanbuf[:, 0:2 * T * L4.W], 0.0))
            dve.sem_inc(L4.s_rows, 2)
            edge_loop_sum(L4)
            dve.wait_ge(L4.s_last, 32)
            mend_sums(L4, 0, FEAT)
            dve.sem_inc(L4.s_mend, 1)
            collect(L4)
            a4 = node_rows(L4)
            link(v.tensor_tensor(a4, a4, bc(has[:, :].unsqueeze(2), [P, K, FEAT]), ALU.mult))
            link(v.tensor_tensor(a4, a4, tab3(FEAT), ALU.add))
            link(v.tensor_tensor(xs3, xs3, bc(b3b[:, :].unsqueeze(1), [P, K, FEAT]), ALU.add))
            add_sums(L4, nt[:, 1, :])
            dve.sem_inc(s_fin, 1)


_INS = ["x", "src", "dst", "edge_attr_16", "edge_type_90", "L0_gnn_W1", "L0_gnn_a_src1", "L0_gnn_a_dst1", "L0_gnn_b1",
        "L0_gnn_W2", "L0_gnn_a_src2", "L0_gnn_a_dst2", "L0_gnn_b2", "L0_gnn_Wf", "L0_gnn_bf", "L2_gnn_Ws", "L2_gnn_Wa",
        "L2_gnn_weight", "L2_gnn_w_comp", "L3_gnn_W", "L3_gnn_b"]


def kernel(**inputs):
    import numpy as _np
    import concourse.bacc as _bacc
    from concourse import mybir as _mybir
    from concourse.bass_utils import run_bass_kernel_spmd as _run

    nc = _bacc.Bacc("TRN2", target_bir_lowering=False, num_devices=1)
    arrays, args = {}, []
    for name in _INS:
        a = _np.ascontiguousarray(inputs[name])
        arrays[f"in_{name}_dram"] = a
        args.append(nc.dram_tensor(f"in_{name}_dram", a.shape, _mybir.dt.from_np(a.dtype), kind="ExternalInput").ap())
    shape = inputs["x"].shape
    args.append(nc.dram_tensor("out_0_dram", shape, _mybir.dt.from_np(_np.dtype("float32")), kind="ExternalOutput").ap())
    gnn_kernel(nc, *args)
    r = _run(nc, [arrays], core_ids=[0])
    return r.results[0]["out_0_dram"]
```
